# Optimizing a Trainium2 kernel written in Bass

```python
import numpy as np
import jax
import jax.numpy as jnp

def _softmax(x, axis=-1):
    return jax.nn.softmax(x, axis=axis)

def _gelu(x):
    return jax.nn.gelu(x, approximate=True)

def _silu(x):
    return jax.nn.silu(x)

def _sigmoid(x):
    return jax.nn.sigmoid(x)

def _layernorm(x, axis=-1, eps=1e-05):
    m = jnp.mean(x, axis=axis, keepdims=True)
    v = jnp.var(x, axis=axis, keepdims=True)
    return (x - m) / jnp.sqrt(v + eps)

def _scatter_add(tgt, idx, src, axis=0):
    return tgt.at[idx].add(src)

def _segment_sum(src, seg, n):
    return jax.ops.segment_sum(src, seg, n)
kernel_name = 'mk_seq_postln_d1_jaxref_r8_811099'

def setup_inputs(seed: int=0):
    np.random.seed(seed)
    _w = jnp.asarray

    def _L0_attn_setup():
        import jax, jax.numpy as jnp
        import numpy as np
        import math
        D_MODEL = 128
        N_HEAD = 16
        D_HEAD = D_MODEL // N_HEAD
        D_KMAP = 128
        B, L = (4, 512)

        def _fourier_kernel(x, proj_mat):
            p = jnp.einsum('blhd,dm->blhm', x, proj_mat) / math.sqrt(D_HEAD)
            return jnp.concatenate([jnp.cos(p), jnp.sin(p)], axis=-1) / math.sqrt(D_KMAP)
        key = jax.random.key(seed)
        ks = jax.random.split(key, 10)
        s = 1.0 / math.sqrt(D_MODEL)
        inp = {'x': jax.random.normal(ks[0], (B, L, D_MODEL), dtype=jnp.float32), 'proj_mat': jax.random.normal(ks[1], (D_HEAD, D_KMAP), dtype=jnp.float32), 'Wq': jax.random.uniform(ks[2], (D_MODEL, D_MODEL), minval=-s, maxval=s), 'bq': jax.random.uniform(ks[3], (D_MODEL,), minval=-s, maxval=s), 'Wk': jax.random.uniform(ks[4], (D_MODEL, D_MODEL), minval=-s, maxval=s), 'bk': jax.random.uniform(ks[5], (D_MODEL,), minval=-s, maxval=s), 'Wv': jax.random.uniform(ks[6], (D_MODEL, D_MODEL), minval=-s, maxval=s), 'bv': jax.random.uniform(ks[7], (D_MODEL,), minval=-s, maxval=s), 'Wo': jax.random.uniform(ks[8], (D_MODEL, D_MODEL), minval=-s, maxval=s), 'bo': jax.random.uniform(ks[9], (D_MODEL,), minval=-s, maxval=s)}
        return inp
    _L0_attn_in = _L0_attn_setup()

    def _L0_ffn_setup():
        import jax, jax.numpy as jnp
        import numpy as np
        B, S, D = (4, 256, 128)
        EXP = 4
        H = EXP * D
        E = 8
        TOP_K = 2
        key = jax.random.key(seed)
        ks = jax.random.split(key, 8)
        scale1 = 1.0 / np.sqrt(D)
        scale2 = 1.0 / np.sqrt(H)
        x = jax.random.normal(ks[0], (B, S, D), dtype=jnp.float32)
        W1 = jax.random.uniform(ks[1], (E, D, H), jnp.float32, -scale1, scale1)
        b1 = jax.random.uniform(ks[2], (E, H), jnp.float32, -scale1, scale1)
        W2 = jax.random.uniform(ks[3], (E, H, D), jnp.float32, -scale2, scale2)
        b2 = jax.random.uniform(ks[4], (E, D), jnp.float32, -scale2, scale2)
        Wr = jax.random.uniform(ks[5], (D, E), jnp.float32, -scale1, scale1)
        br = jax.random.uniform(ks[6], (E,), jnp.float32, -scale1, scale1)
        return {'input_emb': x, 'W1': W1, 'b1': b1, 'W2': W2, 'b2': b2, 'Wr': Wr, 'br': br}
    _L0_ffn_in = _L0_ffn_setup()
    _d = {'L0_attn_x': _L0_attn_in['x'], 'L0_attn_proj_mat': _L0_attn_in['proj_mat'], 'L0_attn_Wq': _L0_attn_in['Wq'], 'L0_attn_bq': _L0_attn_in['bq'], 'L0_attn_Wk': _L0_attn_in['Wk'], 'L0_attn_bk': _L0_attn_in['bk'], 'L0_attn_Wv': _L0_attn_in['Wv'], 'L0_attn_bv': _L0_attn_in['bv'], 'L0_attn_Wo': _L0_attn_in['Wo'], 'L0_attn_bo': _L0_attn_in['bo'], 'L0_ffn_W1': _L0_ffn_in['W1'], 'L0_ffn_b1': _L0_ffn_in['b1'], 'L0_ffn_W2': _L0_ffn_in['W2'], 'L0_ffn_b2': _L0_ffn_in['b2'], 'L0_ffn_Wr': _L0_ffn_in['Wr'], 'L0_ffn_br': _L0_ffn_in['br']}
    _x0 = _d['L0_attn_x']
    _d['L0_attn_x'] = jax.random.normal(jax.random.fold_in(jax.random.key(seed), 1), (8, 512, 128), dtype=_x0.dtype)
    del _x0
    return _d

def reference(L0_attn_x, L0_attn_proj_mat, L0_attn_Wq, L0_attn_bq, L0_attn_Wk, L0_attn_bk, L0_attn_Wv, L0_attn_bv, L0_attn_Wo, L0_attn_bo, L0_ffn_W1, L0_ffn_b1, L0_ffn_W2, L0_ffn_b2, L0_ffn_Wr, L0_ffn_br):

    def _L0_attn_ref(x, proj_mat, Wq, bq, Wk, bk, Wv, bv, Wo, bo):
        import jax, jax.numpy as jnp
        import numpy as np
        import math
        D_MODEL = 128
        N_HEAD = 16
        D_HEAD = D_MODEL // N_HEAD
        D_KMAP = 128
        B, L = (4, 512)

        def _fourier_kernel(x, proj_mat):
            p = jnp.einsum('blhd,dm->blhm', x, proj_mat) / math.sqrt(D_HEAD)
            return jnp.concatenate([jnp.cos(p), jnp.sin(p)], axis=-1) / math.sqrt(D_KMAP)
        Bv, Lv, _ = x.shape
        q = (x @ Wq.T + bq).reshape(Bv, Lv, N_HEAD, D_HEAD)
        k = (x @ Wk.T + bk).reshape(Bv, Lv, N_HEAD, D_HEAD)
        v = (x @ Wv.T + bv).reshape(Bv, Lv, N_HEAD, D_HEAD)
        q_prime = _fourier_kernel(q, proj_mat)
        k_prime = _fourier_kernel(k, proj_mat)
        kv = jnp.einsum('blhm,blhd->bhmd', k_prime, v)
        out = jnp.einsum('blhm,bhmd->blhd', q_prime, kv)
        out = out.reshape(Bv, Lv, D_MODEL)
        return out @ Wo.T + bo

    def _L0_ffn_ref(input_emb, W1, b1, W2, b2, Wr, br):
        import jax, jax.numpy as jnp
        import numpy as np
        B, S, D = (4, 256, 128)
        EXP = 4
        H = EXP * D
        E = 8
        TOP_K = 2
        logits = jnp.einsum('bsd,de->bse', input_emb, Wr) + br
        route_w = jax.nn.softmax(logits, axis=-1)
        _, topk_idx = jax.lax.top_k(route_w, TOP_K)
        mask = jax.nn.one_hot(topk_idx, E, dtype=route_w.dtype).sum(-2)
        routed = route_w * mask
        routed = routed / routed.sum(axis=-1, keepdims=True)
        h = jax.nn.relu(jnp.einsum('bsd,edh->ebsh', input_emb, W1) + b1[:, None, None, :])
        expert_out = jnp.einsum('ebsh,ehd->ebsd', h, W2) + b2[:, None, None, :]
        return jnp.einsum('bse,ebsd->bsd', routed, expert_out)
    x = L0_attn_x
    x = _layernorm(x + _L0_attn_ref(x, L0_attn_proj_mat, L0_attn_Wq, L0_attn_bq, L0_attn_Wk, L0_attn_bk, L0_attn_Wv, L0_attn_bv, L0_attn_Wo, L0_attn_bo), axis=-1)
    x = _layernorm(x + _L0_ffn_ref(x, L0_ffn_W1, L0_ffn_b1, L0_ffn_W2, L0_ffn_b2, L0_ffn_Wr, L0_ffn_br), axis=-1)
    return x

_drawn_inputs = setup_inputs


def setup_inputs(seed=0):
    import zlib

    import numpy as np

    out = dict(_drawn_inputs(seed))
    spreads = {}
    factors = {'L0_attn_bq': 3.339,
     'L0_attn_bk': 2.935,
     'L0_attn_bo': 7.401,
     'L0_ffn_b1': 3.505,
     'L0_ffn_b2': 3.053}
    for name, (base, spread) in spreads.items():
        noise = np.random.default_rng([zlib.crc32(name.encode()), seed]).standard_normal(out[name].shape)
        drawn = base * np.exp(spread * noise) if base else spread * noise
        out[name] = jnp.asarray(drawn.astype(out[name].dtype))
    for name, factor in factors.items():
        out[name] = (out[name] * factor).astype(out[name].dtype)
    return out
```

```python
import math
from contextlib import ExitStack

import concourse.bass as bass
from concourse import mybir

F32 = mybir.dt.float32
BF16 = mybir.dt.bfloat16
F16 = mybir.dt.float16
ALU = mybir.AluOpType
ACT = mybir.ActivationFunctionType
AX = mybir.AxisListType

P = 128
BATCH, LEN = 8, 512
LT = LEN // P
TILES = BATCH * LT
HEADS, DH = 16, 8
HG = 4
G = HEADS // HG
PADH = P // G
FEAT = 128
SPL = 3
STK = SPL * SPL * DH
EXP, HID, HT = 8, 512, 4
UNITS = 16
UC = 1024
CHUNK = 2 * UC
RING = 4
N_LOADS = 9 + SPL * SPL + 2 * LT
N_WLOADS = BATCH + 6
N_SETUP = 9
RT_LOGITS = 14
SLOT = [0, 1, 2] * 5 + [1]
POOL_SQ = (1, 4, 6, 9, 12, 14)
TURN = 1.0 / (2.0 * math.pi * math.sqrt(DH))
MAGIC = 12582912.0
TWO_PI = 6.2831850051879883
EPS = 1e-5
KV_SCALE = 1.0 / FEAT
BIG = 1e37


def slot_prev(u):
    for d in range(1, UNITS + 1):
        if SLOT[(u - d) % UNITS] == SLOT[u]:
            return d


def before(u, pool):
    return sum((x in POOL_SQ) == pool for x in range(u))


def build(nc, x, proj, Wq, bq, Wk, bk, Wv, bv, Wo, bo, W1, b1, W2, b2, Wr, br,
          c_ident, c_negi, c_mask, c_rank, out):
    parts_dram = nc.dram_tensor("parts_dram", [BATCH, 2, SPL, P, LEN], BF16).ap()
    x_rows = x.rearrange("b (t p) d -> b p t d", p=P)
    out_rows = out.rearrange("b (t p) d -> b p t d", p=P)

    ctx = ExitStack()
    with ctx:
        def sb(name, shape, dt=F32):
            return ctx.enter_context(nc.sbuf_tensor(name, shape, dt))

        def sem(name):
            return ctx.enter_context(nc.semaphore(name))

        ident = sb("ident", [P, P])
        negi = sb("negi", [P, P], F16)
        mask = sb("mask", [STK, SPL])
        ones = sb("ones", [P, 2])
        w_raw = sb("w_raw", [P, 4, P])
        wo_pad = sb("wo_pad", [P, HG, G, PADH])
        wT = sb("wT", [P, 3, P])
        woT = sb("woT", [P, HG, P])
        bqk = sb("bqk", [P, 2])
        bqk_t = sb("bqk_t", [P, 2])
        bv_raw = sb("bv_raw", [P, LT, P])
        bv_bc = sb("bv_bc", [P, LT, P])
        bo_bc = sb("bo_bc", [P, LT, P])
        pr = sb("pr", [STK, 3, FEAT])
        prb = sb("prb", [STK, 3, FEAT], BF16)
        proj_stk = sb("proj_stk", [STK, FEAT], BF16)
        w2_s = sb("w2_s", [P, EXP, HT, P])
        wr_s = sb("wr_s", [P, EXP])
        br_bc = sb("br_bc", [P, EXP])
        rank = sb("rank", [P, EXP])
        b1_raw = sb("b1_raw", [EXP * HT, P])
        b1_s = sb("b1_s", [P, EXP * HT])
        b2_s = sb("b2_s", [EXP, P])
        eps_t = sb("eps_t", [P, LT])
        half_t = sb("half_t", [P, LT])
        x_all = sb("x_all", [P, TILES, P])
        x_in = sb("x_in", [P, LT, P])
        xT = sb("xT", [P, LEN])
        qk_f = sb("qk_f", [P, 2, LEN])
        parts = sb("parts", [P, 2, SPL, LEN], BF16)
        stk = sb("stk", [STK, 2, HG, G, LEN], BF16)
        v_pad = sb("v_pad", [P, LT * HEADS, PADH])
        turns = sb("turns", [P, 2, UC], F16)
        feats = sb("feats", [P, RING, 2, CHUNK])
        kvT = sb("kvT", [P, 2, FEAT])
        c_sum = sb("c_sum", [P, HG])
        v_sum = sb("v_sum", [P, 1])
        kv = sb("kv", [P, 2, P])
        outT = sb("outT", [P, HG, LEN])
        y = sb("y", [P, LT, P])
        stats = sb("stats", [P, LT, 6])
        mv = sb("mv", [P, LT, 2])
        rstd = sb("rstd", [P, LT])
        fflat = feats[:, :, :, :].rearrange("p a b c -> p (a b c)")
        w1_s = fflat[:, 0:4096].rearrange("p (e h) -> p e h", e=EXP)
        xnT = fflat[:, 4096:8192]
        hT = fflat[:, 8192:8192 + 2 * 4 * 512].rearrange("p (r j n) -> p r j n", r=2, j=HT)
        rt = fflat[:, 12288:12288 + 8 * 256].rearrange("p (k t e) -> p k t e", k=8, t=TILES)
        small = fflat[:, 14336:14336 + 8 * 32].rearrange("p (k t) -> p k t", k=8)
        gT = fflat[0:EXP, 14848:14848 + LEN]
        gates = rt[:, 4, :, :]
        g_now = sb("g_now", [P, LT, EXP])
        d_top, w_exp = small[:, 3:5, :], small[:, 5:7, :]

        ang = ctx.enter_context(nc.psum_tensor("ang", [P, 3, UC], F32))
        misc = ctx.enter_context(nc.psum_tensor("misc", [P, 2, 512], F32))

        h_bank = [ang[:, i // 2, (i % 2) * 512:(i % 2) * 512 + 512] for i in range(HT)]
        e_bank = [ang[:, 2, i * 512:(i + 1) * 512] for i in range(2)]

        s = {n: sem(n) for n in (
            "loads", "raw_T", "raw_ev", "pad_ok", "setup", "xin_in", "angles", "rounded", "reduced", "sines",
            "sq_v", "sq_p", "xT_mm", "xT_ev", "q_mm", "q_ev", "k_mm", "k_ev", "v_mm", "v_ev",
            "kvT_mm", "kvT_ev", "kv_mm", "kv_ev", "csum", "out_mm", "out_ev", "wo_mm", "y_ok", "bo_ok",
            "ln_stat", "ln_aggr", "ln_eps", "ln_pow", "xn_ok", "split", "parts_out", "moe_in", "xnT_mm", "xnT_ev",
            "lg_mm", "b1_ok", "rt", "rt_exp", "gates_ok", "h_mm", "h_act", "h_dve", "e_mm", "e_free", "e_sum",
            "gT_mm", "gT_ev", "gb_mm", "gb_ok", "done_out", "fin_ok", "wload", "vsum", "v_zero", "held",
        )}
        stk_in = [[sem(f"stk_in{side}{g}") for g in range(HG)] for side in range(2)]
        block = ctx.enter_context(nc.Block())

        def wait(eng, name, per, b, off):
            sm = s[name] if isinstance(name, str) else name
            if isinstance(b, int):
                if per * b + off > 0:
                    eng.wait_ge(sm, per * b + off)
            else:
                eng.wait_ge(sm, b * per + off)

        def hold(eng, name, per, b, off):
            wait(eng, name, per, b, off)
            if not isinstance(b, int):
                eng.sem_inc(s["held"], 1)

        def sequences(eng, body):
            body(0)
            with eng.Fori(1, BATCH - 1) as b:
                body(b)
            body(BATCH - 1)

        @block.sync
        def _(sp):
            n = 0
            sp.dma_start(x_in[:, :, :], x_rows[0]).then_inc(s["xin_in"], 16)
            for dst, src in (
                (ident[:, :], c_ident), (w_raw[:, 0, :], Wk), (w_raw[:, 1, :], Wq), (w_raw[:, 2, :], Wv),
                (w_raw[:, 3, :], Wo), (bqk[:, 0:1], bk.rearrange("(p o) -> p o", o=1)),
                (bqk[:, 1:2], bq.rearrange("(p o) -> p o", o=1)),
                (negi[:, :], c_negi), (mask[:, :], c_mask),
            ):
                sp.dma_start(dst, src).then_inc(s["loads"], 16)
                n += 1
            for r in range(SPL * SPL):
                sp.dma_start(pr[r * DH:(r + 1) * DH, 0, :], proj).then_inc(s["loads"], 16)
                n += 1
            for t in range(LT):
                sp.dma_start(bv_raw[:, t, :], bv.partition_broadcast(P)).then_inc(s["loads"], 16)
                sp.dma_start(bo_bc[:, t, :], bo.partition_broadcast(P)).then_inc(s["loads"], 16)
                n += 2
            assert n == N_LOADS

            def stack(b):
                def write(side):
                    hold(sp, "split", 8, b, 4 * side + 4)
                    dst = parts_dram[b, side].rearrange("i r n -> r i n")
                    sp.dma_start(dst, parts[:, side, :, :]).then_inc(s["parts_out"], 16)
                    hold(sp, "parts_out", 32, b, 16 * side + 16)

                def read(side, hg):
                    hold(sp, "angles", UNITS, b, 4 * hg + 2 * side + 2 - UNITS)
                    for i in range(SPL):
                        src = parts_dram[b, side, i, hg * 32:hg * 32 + 32, :].rearrange("(g d) n -> d g n", g=G)
                        for j in range(SPL):
                            r = (i * SPL + j) * DH
                            sp.dma_start(stk[r:r + DH, side, hg, :, :], src).then_inc(stk_in[side][hg], 16)

                write(0)
                read(0, 0)
                write(1)
                read(1, 0)
                for hg in range(1, HG):
                    read(0, hg)
                    read(1, hg)

            def load_x(b):
                hold(sp, "xT_mm", 1, b, 0)
                sp.dma_start(x_in[:, :, :], x_rows[b]).then_inc(s["xin_in"], 16)

            stack(0)
            load_x(1)
            for t in range(BATCH):
                sp.dma_start(x_all[:, t * LT:(t + 1) * LT, :], x_rows[t]).then_inc(s["wload"], 16)
            sp.dma_start(w2_s[:, :, :, :], W2.rearrange("e (j p) d -> p e j d", p=P)).then_inc(s["wload"], 16)
            sp.dma_start(wr_s[:, :], Wr).then_inc(s["wload"], 16)
            sp.dma_start(br_bc[:, :], br.partition_broadcast(P)).then_inc(s["wload"], 16)
            sp.dma_start(rank[:, :], c_rank.partition_broadcast(P)).then_inc(s["wload"], 16)
            sp.dma_start(b1_raw[:, :], b1.rearrange("e (j p) -> (e j) p", p=P)).then_inc(s["wload"], 16)
            sp.dma_start(b2_s[:, :], b2).then_inc(s["wload"], 16)
            stack(1)
            load_x(2)
            with sp.Fori(2, BATCH - 1) as b:
                stack(b)
                load_x(b + 1)
            stack(BATCH - 1)
            wait(sp, "out_mm", HG, BATCH - 1, HG)
            wait(sp, "kvT_mm", HG, BATCH - 1, HG)
            sp.dma_start(w1_s, W1.rearrange("e d h -> d e h")).then_inc(s["moe_in"], 16)
            with sp.Fori(0, BATCH) as b:
                hold(sp, "fin_ok", 1, b, 1)
                sp.dma_start(out_rows[b], x_all[:, bass.ds(b * LT, LT), :]).then_inc(s["done_out"], 16)
            sp.wait_ge(s["done_out"], 16 * BATCH)

        @block.tensor
        def _(pe):
            pe.wait_ge(s["loads"], 16 * N_LOADS)
            for i in range(3):
                mm = pe.transpose(misc[:, 0, i * P:(i + 1) * P], w_raw[:, i, :], ident[:, :])
            mm.then_inc(s["raw_T"], 1)
            pe.wait_ge(s["pad_ok"], 2)
            for i in range(HG):
                mm = pe.transpose(misc[:, 1, i * P:(i + 1) * P],
                                  wo_pad[:, i, :, :].rearrange("p g w -> p (g w)"), ident[:, :])
            mm.then_inc(s["raw_T"], 1)

            def x_T(b):
                wait(pe, "xin_in", 16, b, 16)
                if isinstance(b, int) and b == 0:
                    pe.wait_ge(s["raw_ev"], 2)
                else:
                    wait(pe, "v_ev", 1, b, 0)
                for t in range(LT):
                    mm = pe.transpose(misc[:, 0, t * P:(t + 1) * P], x_in[:, t, :], ident[:, :])
                mm.then_inc(s["xT_mm"], 1)

            def project(side, bank, free, b):
                name = "kq"[side]
                wait(pe, "xT_ev", 1, b, 1)
                if free:
                    wait(pe, *free)
                pe.matmul(misc[:, bank, :], wT[:, side, :], xT[:, :], start=True, stop=True)\
                    .then_inc(s[name + "_mm"], 1)

            x_T(0)
            project(0, 1, None, 0)
            project(1, 0, None, 0)

            def angles(b, u):
                c, half = u // 2, u % 2
                hg, side = c // 2, c % 2
                if half == 0:
                    wait(pe, stk_in[side][hg], 16 * SPL * SPL, b, 16 * SPL * SPL)
                wait(pe, "sines", UNITS, b, u - slot_prev(u) + 1)
                a = ang[:, SLOT[u], :]
                if side == 0:
                    for t in range(2):
                        for g in range(G):
                            at = (t * G + g) * FEAT
                            tok = (2 * half + t) * P
                            mm = pe.matmul(a[:, at:at + FEAT], stk[:, 0, hg, g, tok:tok + P], proj_stk[:, :],
                                           start=(g == 0), stop=False, skip_group_check=True)
                else:
                    for t in range(2):
                        mm = pe.matmul(a[:, t * 512:(t + 1) * 512], proj_stk[:, :],
                                       stk[:, 1, hg, 2 * half + t, :], start=True, stop=False,
                                       skip_group_check=True)
                mm.then_inc(s["angles"], 1)

            def reduce_turns(b, u):
                wait(pe, "rounded", UNITS, b, u + 1)
                for t in range(2):
                    mm = pe.matmul(ang[:, SLOT[u % UNITS], t * 512:(t + 1) * 512], negi[:, :],
                                   turns[:, u % 2, t * 512:(t + 1) * 512], start=False, stop=True,
                                   skip_group_check=True)
                mm.then_inc(s["reduced"], 1)

            def squared(b, u):
                wait(pe, "sq_v", UNITS - len(POOL_SQ), b, before(u + 1, False))
                wait(pe, "sq_p", len(POOL_SQ), b, before(u + 1, True))

            def kv_product(b, hg, free):
                c = 2 * hg
                squared(b, 2 * c + 1)
                wait(pe, "v_ev", 1, b, 1)
                wait(pe, *free)
                f = feats[:, c % RING, :, :]
                for t in range(LT):
                    for g in range(G):
                        at = (t * G + g) * FEAT
                        o = misc[32 * g:32 * g + 32, 0, :]
                        w = v_pad[:, t * HEADS + hg * G + g, :]
                        pe.matmul(o[:, 0:2 * FEAT].rearrange("p (a m) -> p a m", a=2), w, f[:, :, at:at + FEAT],
                                  start=(t == 0), stop=False, skip_group_check=True)
                    for g in range(G):
                        o = misc[32 * g:32 * g + 32, 0, :]
                        w = v_pad[:, t * HEADS + hg * G + g, :]
                        mm = pe.matmul(o[:, 2 * FEAT:2 * FEAT + 2], w, ones[:, :],
                                       start=False, stop=(t == LT - 1), skip_group_check=True)
                mm.then_inc(s["kvT_mm"], 1)

            def kv_turn(b, hg, free):
                wait(pe, "kvT_ev", HG, b, hg + 1)
                wait(pe, *free)
                for a in range(2):
                    mm = pe.transpose(misc[:, 1, a * P:(a + 1) * P], kvT[:, a, :], ident[:, :])
                mm.then_inc(s["kv_mm"], 1)

            def out_product(b, hg, free):
                c = 2 * hg + 1
                squared(b, 2 * c + 1)
                wait(pe, "kv_ev", HG, b, hg + 1)
                wait(pe, *free)
                for a in range(2):
                    for g in range(G):
                        mm = pe.matmul(misc[32 * g:32 * g + 32, 0, :], kv[:, a, 32 * g:32 * g + 32],
                                       feats[:, c % RING, a, g * LEN:(g + 1) * LEN],
                                       start=(a == 0), stop=(a == 1), skip_group_check=True)
                mm.then_inc(s["out_mm"], 1)

            def v_product(b):
                wait(pe, "kvT_ev", HG, b, 0)
                if isinstance(b, int) and b == 0:
                    pe.wait_ge(s["q_ev"], 1)
                    pe.wait_ge(s["xT_ev"], 1)
                for t in range(LT):
                    mm = pe.matmul(misc[:, 0, t * P:(t + 1) * P], xT[:, t * P:(t + 1) * P], wT[:, 2, :],
                                   start=True, stop=True)
                mm.then_inc(s["v_mm"], 1)

            def wo_product(b):
                wait(pe, "out_ev", HG, b, HG)
                for t in range(LT):
                    for hg in range(HG):
                        mm = pe.matmul(misc[:, 1, t * P:(t + 1) * P], outT[:, hg, t * P:(t + 1) * P],
                                       woT[:, hg, :], start=(hg == 0), stop=(hg == HG - 1))
                mm.then_inc(s["wo_mm"], 1)

            def body(b):
                first = isinstance(b, int) and b == 0
                last = isinstance(b, int) and b == BATCH - 1
                for u in range(UNITS):
                    angles(b, u)
                    if not (first and u == 0):
                        reduce_turns(b, u - 1)
                    if u == 0 and not first:
                        kv_product(b - 1, HG - 1, ("out_ev", HG, b, -1))
                    if u == 1:
                        if not first:
                            kv_turn(b - 1, HG - 1, ("kv_ev", HG, b, -1))
                        v_product(b)
                    if u == 2 and not first:
                        out_product(b - 1, HG - 1, ("v_ev", 1, b, 1))
                    if u == 3 and not last:
                        if not first:
                            wait(pe, "out_ev", HG, b, 0)
                        x_T(b + 1)
                    if u == 4:
                        kv_product(b, 0, ("xT_ev", 1, b, 2) if not last else ("out_ev", HG, b, 0))
                    if u == 5:
                        kv_turn(b, 0, ("k_ev", 1, b, 1) if first else ("kv_ev", HG, b, 0))
                        if not last:
                            project(0, 1, ("kv_ev", HG, b, 1), b + 1)
                    if u == 6:
                        if not first:
                            if last:
                                wait(pe, "kv_ev", HG, b, 1)
                            else:
                                wait(pe, "k_ev", 1, b, 2)
                            wo_product(b - 1)
                        out_product(b, 0, ("kvT_ev", HG, b, 1))
                    if u == 7 and not last:
                        project(1, 0, ("out_ev", HG, b, 1), b + 1)
                    if u == 8:
                        kv_product(b, 1, ("q_ev", 1, b, 2) if not last else ("out_ev", HG, b, 1))
                    if u == 9:
                        kv_turn(b, 1, ("k_ev", 1, b, 2) if first else ("y_ok", 1, b, 0))
                    if u == 10:
                        out_product(b, 1, ("kvT_ev", HG, b, 2))
                    if u == 12:
                        kv_product(b, 2, ("out_ev", HG, b, 2))
                    if u == 13:
                        kv_turn(b, 2, ("kv_ev", HG, b, 2))
                    if u == 14:
                        out_product(b, 2, ("kvT_ev", HG, b, 3))

            pe.wait_ge(s["setup"], N_SETUP)
            sequences(pe, body)
            e = BATCH
            reduce_turns(e, -1)
            kv_product(e - 1, HG - 1, ("out_ev", HG, e, -1))
            kv_turn(e - 1, HG - 1, ("kv_ev", HG, e, -1))
            out_product(e - 1, HG - 1, ("kvT_ev", HG, e, 0))
            pe.wait_ge(s["kv_ev"], HG * e)
            wo_product(e - 1)

            pe.wait_ge(s["wload"], 16 * N_WLOADS)
            pe.wait_ge(s["xn_ok"], BATCH)
            pe.wait_ge(s["sines"], UNITS * BATCH)
            for b in range(BATCH):
                if b >= 2:
                    pe.wait_ge(s["xnT_ev"], b - 1)
                for t in range(LT):
                    mm = pe.transpose(misc[:, b % 2, t * P:(t + 1) * P], x_all[:, b * LT + t, :], ident[:, :])
                mm.then_inc(s["xnT_mm"], 1)
            pe.wait_ge(s["xnT_ev"], BATCH)
            for t in range(TILES):
                mm = pe.matmul(misc[:, 0, t * EXP:(t + 1) * EXP], xnT[:, t * P:(t + 1) * P], wr_s[:, :],
                               start=True, stop=True)
            mm.then_inc(s["lg_mm"], 1)
            pe.transpose(misc[:, 1, 0:EXP * HT], b1_raw[:, :], ident[0:EXP * HT, 0:EXP * HT])\
                .then_inc(s["lg_mm"], 1)
            pe.wait_ge(s["moe_in"], 16)

            for b in range(BATCH):
                pe.wait_ge(s["gates_ok"], 1)
                if b >= 1:
                    pe.wait_ge(s["gT_ev"], b)
                for t in range(LT):
                    mm = pe.transpose(misc[0:EXP, 0, t * P:(t + 1) * P], gates[:, b * LT + t, :], ident[:, :])
                mm.then_inc(s["gT_mm"], 1)
                pe.wait_ge(s["gT_ev"], b + 1)
                if b >= 1:
                    pe.wait_ge(s["gb_ok"], b)
                else:
                    pe.wait_ge(s["b1_ok"], 1)
                for t in range(LT):
                    mm = pe.matmul(misc[:, 1, t * P:(t + 1) * P], gT[:, t * P:(t + 1) * P], b2_s[:, :],
                                   start=True, stop=True)
                mm.then_inc(s["gb_mm"], 1)

            def first_layer(b, e):
                for j in range(HT):
                    if e >= 1:
                        if j < 2:
                            wait(pe, "h_act", 2 * EXP, b, 2 * (e - 1) + j + 1)
                        else:
                            wait(pe, "h_dve", 2 * EXP, b, 2 * (e - 1) + j - 1)
                    pe.matmul(h_bank[j], w1_s[:, e, j * P:(j + 1) * P], xnT[:, bass.ds(b * LEN, LEN)],
                              start=True, stop=True).then_inc(s["h_mm"], 1)

            def second_layer(b, e):
                wait(pe, "h_act", 2 * EXP, b, 2 * e + 2)
                wait(pe, "h_dve", 2 * EXP, b, 2 * e + 2)
                wait(pe, "e_free", EXP, b, e + 1)
                for t in range(LT):
                    for j in range(HT):
                        mm = pe.matmul(e_bank[e % 2][:, t * P:(t + 1) * P], hT[:, e % 2, j, t * P:(t + 1) * P],
                                       w2_s[:, e, j, :], start=(j == 0), stop=(j == HT - 1))
                mm.then_inc(s["e_mm"], 1)

            with pe.Fori(0, BATCH) as b:
                for e in range(EXP):
                    first_layer(b, e)
                    if e >= 1:
                        second_layer(b, e - 1)
                second_layer(b, EXP - 1)

        @block.scalar
        def _(act):
            def out_evac(b, hg):
                wait(act, "out_mm", HG, b, hg + 1)
                wait(act, "csum", HG, b, hg + 1)
                act.activation(outT[:, hg, :], misc[:, 0, :], ACT.Identity, bias=c_sum[:, hg:hg + 1])\
                    .then_inc(s["out_ev"], 1)

            def proj_evac(b, side):
                wait(act, "kq"[side] + "_mm", 1, b, 1)
                wait(act, "split", 8, b, 4 * side - 4)
                act.activation(qk_f[:, side, :], misc[:, 1 - side, :], ACT.Identity,
                               bias=bqk_t[:, side:side + 1], scale=TURN).then_inc(s["kq"[side] + "_ev"], 1)

            def sines(b, u):
                c, half = u // 2, u % 2
                wait(act, "reduced", UNITS, b, u + 1)
                if half == 0:
                    wait(act, ("kvT_mm", "out_mm")[c % 2], HG, b, c // 2 - 1)
                a = ang[:, SLOT[u], :]
                f = feats[:, c % RING, :, half * UC:(half + 1) * UC]
                act.activation(f[:, 0, :], a, ACT.Sin, scale=TWO_PI)
                act.activation(f[:, 1, :], a, ACT.Sin, scale=TWO_PI / 2).then_inc(s["sines"], 1)

            act.wait_ge(s["setup"], 1)
            proj_evac(0, 0)
            proj_evac(0, 1)

            def body(b):
                first = isinstance(b, int) and b == 0
                last = isinstance(b, int) and b == BATCH - 1
                for u in range(UNITS):
                    if u == 2 and not first:
                        out_evac(b - 1, HG - 1)
                    if u in (6, 10, 14):
                        out_evac(b, (u - 6) // 4)
                    if u == 5 and not last:
                        proj_evac(b + 1, 0)
                    if u == 7 and not last:
                        proj_evac(b + 1, 1)
                    sines(b, u)

            sequences(act, body)
            out_evac(BATCH - 1, HG - 1)

            act.wait_ge(s["rt"], RT_LOGITS)
            act.activation(w_exp, d_top, ACT.Exp).then_inc(s["rt_exp"], 1)
            act.wait_ge(s["b1_ok"], 1)
            with act.Fori(0, BATCH) as b:
                for e in range(EXP):
                    for j in range(2):
                        wait(act, "h_mm", EXP * HT, b, e * HT + j + 1)
                        act.activation(hT[:, e % 2, j, :], h_bank[j], ACT.Relu,
                                       bias=b1_s[:, e * HT + j:e * HT + j + 1]).then_inc(s["h_act"], 1)

        @block.vector
        def _(dve):
            dve.memset(wo_pad[:, :, :, :], 0.0).then_inc(s["pad_ok"], 1)
            dve.memset(ones[:, :], 1.0)
            dve.memset(eps_t[:, :], EPS)
            dve.memset(half_t[:, :], -0.5)
            dve.wait_ge(s["loads"], 16 * N_LOADS)
            dve.wait_ge(s["pad_ok"], 1)
            dve.tensor_copy(wo_pad[:, :, :, 0:DH],
                            w_raw[:, 3, :].rearrange("p (a g d) -> p a g d", a=HG, g=G)).then_inc(s["pad_ok"], 1)
            dve.tensor_scalar(bqk_t[:, :], bqk[:, :], TURN, None, ALU.mult).then_inc(s["setup"], 1)
            dve.tensor_scalar(bv_bc[:, :, :], bv_raw[:, :, :], KV_SCALE, None, ALU.mult)
            dve.wait_ge(s["raw_T"], 1)
            dve.tensor_copy(wT[:, :, :].rearrange("p a n -> p (a n)"), misc[:, 0, 0:3 * P]).then_inc(s["raw_ev"], 1)
            dve.wait_ge(s["raw_T"], 2)
            dve.tensor_copy(woT[:, :, :].rearrange("p a n -> p (a n)"), misc[:, 1, :]).then_inc(s["raw_ev"], 1)
            n_set = [1]

            def chain(ins):
                n_set[0] += 1
                ins.then_inc(s["setup"], 1)
                dve.wait_ge(s["setup"], n_set[0])

            def x_evac(b):
                wait(dve, "xT_mm", 1, b, 1)
                dve.tensor_copy(xT[:, :], misc[:, 0, :]).then_inc(s["xT_ev"], 1)

            x_evac(0)
            for i in range(SPL):
                chain(dve.tensor_copy(prb[:, i, :], pr[:, i, :]))
                if i < SPL - 1:
                    chain(dve.tensor_tensor(pr[:, i + 1, :], pr[:, i, :], prb[:, i, :], ALU.subtract))
            chain(dve.tensor_scalar(pr[:, 0, :], prb[:, 0, :], mask[:, 0:1], None, ALU.mult))
            chain(dve.scalar_tensor_tensor(out=pr[:, 1, :], in0=prb[:, 1, :], scalar=mask[:, 1:2],
                                           in1=pr[:, 0, :], op0=ALU.mult, op1=ALU.add))
            chain(dve.scalar_tensor_tensor(out=proj_stk[:, :], in0=prb[:, 2, :], scalar=mask[:, 2:3],
                                           in1=pr[:, 1, :], op0=ALU.mult, op1=ALU.add))
            assert n_set[0] == N_SETUP

            def round_turns(b, u):
                wait(dve, "angles", UNITS, b, u + 1)
                wait(dve, "reduced", UNITS, b, u - 1)
                dve.tensor_scalar(turns[:, u % 2, :], ang[:, SLOT[u], :], MAGIC, -MAGIC, ALU.add, ALU.add)\
                    .then_inc(s["rounded"], 1)

            def square(b, u):
                if u % UNITS in POOL_SQ:
                    return
                wait(dve, "sines", UNITS, b, u + 1)
                f = feats[:, (u % UNITS) // 2 % RING, 1, (u % 2) * UC:(u % 2 + 1) * UC]
                dve.tensor_tensor(f, f, f, ALU.mult).then_inc(s["sq_v"], 1)

            def kvT_evac(b, hg):
                wait(dve, "kvT_mm", HG, b, hg + 1)
                m = misc[:, 0, :]
                dve.tensor_copy(v_sum[:, :], m[:, 2 * FEAT:2 * FEAT + 1]).then_inc(s["vsum"], 1)
                dve.tensor_copy(kvT[:, 0, :], m[:, 0:FEAT])
                wait(dve, "vsum", HG, b, hg + 1)
                dve.tensor_scalar(kvT[:, 1, :], m[:, FEAT:2 * FEAT], -2.0, v_sum[:, 0:1], ALU.mult, ALU.add)\
                    .then_inc(s["kvT_ev"], 1)
                wait(dve, "kvT_ev", HG, b, hg + 1)
                wait(dve, "out_ev", HG, b, hg + 1 - HG)
                dve.tensor_reduce(c_sum[:, hg:hg + 1], kvT[:, 1, :], AX.X, ALU.add).then_inc(s["csum"], 1)

            def kv_evac(b, hg):
                wait(dve, "kv_mm", HG, b, hg + 1)
                dve.tensor_copy(kv[:, 0, :], misc[:, 1, 0:P])
                dve.tensor_scalar(kv[:, 1, :], misc[:, 1, P:2 * P], -2.0, None, ALU.mult).then_inc(s["kv_ev"], 1)

            def v_evac(b):
                wait(dve, "v_mm", 1, b, 1)
                dve.scalar_tensor_tensor(out=v_pad[:, :, 0:DH],
                                         in0=misc[:, 0, :].rearrange("p (a d) -> p a d", d=DH), scalar=KV_SCALE,
                                         in1=bv_bc[:, :, :].rearrange("p t (h d) -> p (t h) d", d=DH),
                                         op0=ALU.mult, op1=ALU.add).then_inc(s["v_ev"], 1)

            def moments(n, base):
                for t in range(LT):
                    ins = dve.bn_stats(stats[:, t, :], y[:, t, :])
                ins.then_inc(s["ln_stat"], 1)
                hold(dve, "ln_stat", 1, n, base + 1)
                for t in range(LT):
                    ins = dve.bn_aggr(mv[:, t, :], stats[:, t, :])
                ins.then_inc(s["ln_aggr"], 1)

            def normalize(n, base, b, done):
                wait(dve, "ln_pow", 1, n, base + 1)
                for t in range(LT):
                    ins = dve.tensor_scalar(x_tile(b, t), y[:, t, :], mv[:, t, 0:1], rstd[:, t:t + 1],
                                            ALU.subtract, ALU.mult)
                ins.then_inc(s[done], 1)

            def x_tile(b, t):
                if isinstance(b, int):
                    return x_all[:, b * LT + t, :]
                return x_all[:, bass.ds(b * LT + t, 1), :].rearrange("p a d -> p (a d)")

            def residual(b):
                wait(dve, "wo_mm", 1, b, 1)
                dve.wait_ge(s["bo_ok"], BATCH)
                dve.wait_ge(s["wload"], 16 * N_WLOADS)
                xb = x_all[:, b * LT:(b + 1) * LT, :] if isinstance(b, int) else x_all[:, bass.ds(b * LT, LT), :]
                dve.tensor_tensor(y[:, :, :], misc[:, 1, :].rearrange("p (t d) -> p t d", t=LT), xb, ALU.add)\
                    .then_inc(s["y_ok"], 1)
                wait(dve, "y_ok", 1, b, 1)
                moments(b, 0)

            def body(b):
                first = isinstance(b, int) and b == 0
                last = isinstance(b, int) and b == BATCH - 1
                for u in range(UNITS):
                    round_turns(b, u)
                    if not (first and u < 2):
                        square(b, u - 2)
                    if u == 0 and not first:
                        kvT_evac(b - 1, HG - 1)
                    if u == 1:
                        if not first:
                            kv_evac(b - 1, HG - 1)
                        v_evac(b)
                    if u == 3 and not last:
                        x_evac(b + 1)
                    if u in (4, 8, 12):
                        kvT_evac(b, u // 4 - 1)
                    if u in (5, 9, 13):
                        kv_evac(b, u // 4 - 1)
                    if u == 6 and not first:
                        residual(b - 1)
                    if u == 7 and not first:
                        normalize(b - 1, 0, b - 1, "xn_ok")

            sequences(dve, body)
            e = BATCH
            square(e, -2)
            square(e, -1)
            kvT_evac(e - 1, HG - 1)
            kv_evac(e - 1, HG - 1)
            residual(e - 1)
            normalize(e - 1, 0, e - 1, "xn_ok")

            for b in range(BATCH):
                dve.wait_ge(s["xnT_mm"], b + 1)
                dve.tensor_copy(xnT[:, b * LEN:(b + 1) * LEN], misc[:, b % 2, :]).then_inc(s["xnT_ev"], 1)
            n_rt = [0]

            def rchain(ins):
                n_rt[0] += 1
                ins.then_inc(s["rt"], 1)
                dve.wait_ge(s["rt"], n_rt[0])

            def per_tile(v):
                return v.unsqueeze(2).broadcast_to([P, TILES, EXP])

            def over_tiles(v):
                return v.unsqueeze(1).broadcast_to([P, TILES, EXP])

            L, eq, hot1, hot2 = (rt[:, k, :, :] for k in range(4))
            dve.wait_ge(s["lg_mm"], 2)
            rchain(dve.tensor_tensor(L, misc[:, 0, 0:TILES * EXP].rearrange("p (t e) -> p t e", e=EXP),
                                     over_tiles(br_bc[:, :]), ALU.add))
            dve.tensor_copy(b1_s[:, :], misc[:, 1, 0:EXP * HT]).then_inc(s["b1_ok"], 1)

            def top(hot, m, r):
                rchain(dve.tensor_reduce(m, L, AX.X, ALU.max))
                rchain(dve.tensor_tensor(eq, L, per_tile(m), ALU.is_equal))
                rchain(dve.tensor_tensor(eq, eq, over_tiles(rank[:, :]), ALU.mult))
                rchain(dve.tensor_reduce(r, eq, AX.X, ALU.max))
                rchain(dve.tensor_tensor(hot, over_tiles(rank[:, :]), per_tile(r), ALU.is_equal))

            m1, m2, r_top = small[:, 0, :], small[:, 1, :], small[:, 2, :]
            top(hot1, m1, r_top)
            rchain(dve.scalar_tensor_tensor(out=L, in0=hot1, scalar=-BIG, in1=L, op0=ALU.mult, op1=ALU.add))
            top(hot2, m2, r_top)
            rchain(dve.tensor_tensor(small[:, 3, :], m1, m1, ALU.subtract))
            rchain(dve.tensor_tensor(small[:, 4, :], m2, m1, ALU.subtract))
            assert n_rt[0] == RT_LOGITS
            dve.wait_ge(s["rt_exp"], 1)
            g1, g2, tot = small[:, 5, :], small[:, 6, :], small[:, 7, :]
            rchain(dve.tensor_tensor(tot, g1, g2, ALU.add))
            rchain(dve.reciprocal(tot, tot))
            rchain(dve.tensor_tensor(g1, g1, tot, ALU.mult))
            rchain(dve.tensor_tensor(g2, g2, tot, ALU.mult))
            rchain(dve.tensor_tensor(hot1, hot1, per_tile(g1), ALU.mult))
            rchain(dve.tensor_tensor(hot2, hot2, per_tile(g2), ALU.mult))
            dve.tensor_tensor(gates, hot1, hot2, ALU.add).then_inc(s["gates_ok"], 1)
            for b in range(BATCH):
                dve.wait_ge(s["gT_mm"], b + 1)
                if b >= 1:
                    dve.wait_ge(s["gb_mm"], b)
                dve.tensor_copy(gT, misc[0:EXP, 0, :]).then_inc(s["gT_ev"], 1)
                dve.wait_ge(s["gb_mm"], b + 1)
                xb = x_all[:, b * LT:(b + 1) * LT, :]
                dve.tensor_tensor(xb, misc[:, 1, :].rearrange("p (t d) -> p t d", t=LT), xb, ALU.add)\
                    .then_inc(s["gb_ok"], 1)
            dve.wait_ge(s["gates_ok"], 1)
            dve.wait_ge(s["gb_ok"], BATCH)
            dve.memset(v_sum[:, :], 0.0).then_inc(s["e_free"], 1)
            dve.memset(g_now[:, :, :], 0.0).then_inc(s["e_free"], 1)
            dve.wait_ge(s["e_free"], 2)

            def hidden(b, e):
                for j in range(2, HT):
                    wait(dve, "h_mm", EXP * HT, b, e * HT + j + 1)
                    dve.tensor_scalar(hT[:, e % 2, j, :], h_bank[j], b1_s[:, e * HT + j:e * HT + j + 1], 0.0,
                                      ALU.add, ALU.max).then_inc(s["h_dve"], 1)

            def add_expert(b, e):
                wait(dve, "e_mm", EXP, b, e + 1)
                wait(dve, "e_sum", EXP + 1, b, e + 1)
                for t in range(LT):
                    src = (x_tile(b, t) if e == 0 else y[:, t, :])
                    ins = dve.scalar_tensor_tensor(out=y[:, t, :], in0=e_bank[e % 2][:, t * P:(t + 1) * P],
                                                   scalar=g_now[:, t, e:e + 1], in1=src, op0=ALU.mult, op1=ALU.add)
                ins.then_inc(s["e_sum"], 1)
                wait(dve, "e_sum", EXP + 1, b, e + 2)
                dve.memset(v_sum[:, :], 0.0).then_inc(s["e_free"], 1)

            with dve.Fori(0, BATCH) as b:
                dve.tensor_copy(g_now[:, :, :], gates[:, bass.ds(b * LT, LT), :]).then_inc(s["e_sum"], 1)
                for e in range(EXP):
                    hidden(b, e)
                    if e >= 1:
                        add_expert(b, e - 1)
                add_expert(b, EXP - 1)
                moments(b, BATCH)
                normalize(b, BATCH, b, "fin_ok")

        @block.gpsimd
        def _(pool):
            pool.memset(v_pad[:, :, :], 0.0).then_inc(s["v_zero"], 1)

            def split(b, side):
                wait(pool, "kq"[side] + "_ev", 1, b, 1)
                hold(pool, "parts_out", 32, b, 16 * side - 16)
                f = qk_f[:, side, :]
                p = parts[:, side, :, :]
                n = 4 * side
                pool.tensor_copy(p[:, 0, :], f).then_inc(s["split"], 1)
                wait(pool, "split", 8, b, n + 1)
                pool.tensor_tensor(f, f, p[:, 0, :], ALU.subtract).then_inc(s["split"], 1)
                hold(pool, "split", 8, b, n + 2)
                pool.tensor_copy(p[:, 1, :], f).then_inc(s["split"], 1)
                wait(pool, "split", 8, b, n + 3)
                pool.tensor_tensor(p[:, 2, :], f, p[:, 1, :], ALU.subtract).then_inc(s["split"], 1)

            def square(b, u):
                if u % UNITS not in POOL_SQ:
                    return
                wait(pool, "sines", UNITS, b, u + 1)
                f = feats[:, (u % UNITS) // 2 % RING, 1, (u % 2) * UC:(u % 2 + 1) * UC]
                pool.tensor_tensor(f, f, f, ALU.mult).then_inc(s["sq_p"], 1)

            def rsqrt(n, base):
                wait(pool, "ln_aggr", 1, n, base + 1)
                pool.tensor_tensor(rstd[:, :], mv[:, :, 1], eps_t[:, :], ALU.add).then_inc(s["ln_eps"], 1)
                wait(pool, "ln_eps", 1, n, base + 1)
                pool.tensor_tensor(rstd[:, :], rstd[:, :], half_t[:, :], ALU.pow).then_inc(s["ln_pow"], 1)

            split(0, 0)
            split(0, 1)
            pool.wait_ge(s["wload"], 16 * N_WLOADS)

            def body(b):
                first = isinstance(b, int) and b == 0
                last = isinstance(b, int) and b == BATCH - 1
                for u in range(UNITS):
                    if not (first and u < 2):
                        square(b, u - 2)
                    if first and u % 2 == 1:
                        t = u // 2 * LT
                        xb = x_all[:, t:t + LT, :]
                        pool.tensor_tensor(xb, xb, bo_bc[:, :, :], ALU.add).then_inc(s["bo_ok"], 1)
                    if u == 6 and not last:
                        split(b + 1, 0)
                    if u == 7 and not first:
                        rsqrt(b - 1, 0)
                    if u == 8 and not last:
                        split(b + 1, 1)

            sequences(pool, body)
            square(BATCH, -2)
            square(BATCH, -1)
            rsqrt(BATCH - 1, 0)
            with pool.Fori(0, BATCH) as b:
                rsqrt(b, BATCH)


_INS = ["attn_x", "attn_proj_mat", "attn_Wq", "attn_bq", "attn_Wk", "attn_bk", "attn_Wv", "attn_bv", "attn_Wo",
        "attn_bo", "ffn_W1", "ffn_b1", "ffn_W2", "ffn_b2", "ffn_Wr", "ffn_br"]


def constants():
    import numpy as np
    mask = np.zeros((STK, SPL), np.float32)
    for r in range(STK):
        mask[r, r // DH % SPL] = 1.0
    return [np.eye(P, dtype=np.float32), -np.eye(P, dtype=np.float16), mask,
            np.arange(EXP, 0, -1).astype(np.float32)]


def kernel(**inputs):
    import numpy as _np
    import concourse.bacc as _bacc
    from concourse import mybir as _mybir
    from concourse.bass_utils import run_bass_kernel_spmd as _run

    nc = _bacc.Bacc("TRN2", target_bir_lowering=False, num_devices=1)
    arrays, args = {}, []
    every = [(n, _np.ascontiguousarray(inputs["L0_" + n])) for n in _INS]
    every += [(f"const{i}", c) for i, c in enumerate(constants())]
    for name, a in every:
        arrays[name] = a
        args.append(nc.dram_tensor(name, a.shape, _mybir.dt.from_np(a.dtype), kind="ExternalInput").ap())
    args.append(nc.dram_tensor("out", (BATCH, LEN, P), F32, kind="ExternalOutput").ap())
    build(nc, *args)
    r = _run(nc, [arrays], core_ids=[0])
    return r.results[0]["out"]
```

```python
import math
from contextlib import ExitStack

import concourse.bass as bass
from concourse import mybir

F32 = mybir.dt.float32
U32 = mybir.dt.uint32
BF16 = mybir.dt.bfloat16
F16 = mybir.dt.float16
ALU = mybir.AluOpType
ACT = mybir.ActivationFunctionType
AX = mybir.AxisListType

P = 128
BATCH, LEN = 8, 512
LT = LEN // P
TILES = BATCH * LT
HEADS, DH = 16, 8
HG = 4
G = HEADS // HG
PADH = P // G
FEAT = 128
SPL = 3
PADW = PADH + DH
STK = SPL * SPL * DH
EXP, HID, HT = 8, 512, 4
UNITS = 16
UC = 1024
HALF = UNITS // 2
RING = 3
KV_STEP = [3, 4, 5, 7, 8, 9, 10, 11]
N_LOADS = 12
N_WLOADS = BATCH + 12
N_SETUP = 9
POOL_SQ = (1, 3, 4, 6, 8, 10, 12)
TURN = 1.0 / (2.0 * math.pi * math.sqrt(DH))
MAGIC = 12582912.0
TWO_PI = 6.2831850051879883
EPS = 1e-5
KV_SCALE = 1.0 / FEAT
MAGIC_LAST = 0.5 - 1.0 / 256
TOPK = 2
ROWS = BATCH * LEN
REGION = ROWS + P
XW = P + 2
N_TILES = 72
UNROLL = 8
RING_X = UNROLL


def slot(phase, u):
    return (UNITS * phase + u) % RING


def before(u, pool):
    return sum((x in POOL_SQ) == pool for x in range(u))


def build(nc, x, proj, Wq, bq, Wk, bk, Wv, bv, Wo, bo, W1, b1, W2, b2, Wr, br,
          c_ident, c_negi, c_mask, c_iota, c_base, c_tile, c_tri, c_tok, c_pad, out):
    parts_dram = nc.dram_tensor("parts_dram", [BATCH, 2, SPL, P, LEN], BF16).ap()
    routed_dram = nc.dram_tensor("routed_dram", [(EXP + 1) * REGION, XW], F32).ap()
    expert_dram = nc.dram_tensor("expert_dram", [TOPK * ROWS + N_TILES * P, P], F32).ap()
    x_rows = x.rearrange("b (t p) d -> b p t d", p=P)
    out_rows = out.rearrange("b (t p) d -> b p t d", p=P)

    ctx = ExitStack()
    with ctx:
        def sb(name, shape, dt=F32):
            return ctx.enter_context(nc.sbuf_tensor(name, shape, dt))

        def sem(name):
            return ctx.enter_context(nc.semaphore(name))

        ident = sb("ident", [P, P])
        negi = sb("negi", [P, P], F16)
        mask = sb("mask", [STK, SPL])
        ident4 = sb("ident4", [P, P])
        minus_2 = sb("minus_2", [P, P])
        minus_half = sb("minus_half", [P, 2])
        w_raw = sb("w_raw", [P, 4, P])
        wo_perm = sb("wo_perm", [P, P])
        wT = sb("wT", [P, 3, P])
        woT = sb("woT", [P, P])
        bqk = sb("bqk", [2, P])
        bqk_p = sb("bqk_p", [2, P])
        bqk_t = sb("bqk_t", [P, 2])
        bv_raw = sb("bv_raw", [P, P])
        bv_bc = sb("bv_bc", [P, LT, P])
        bo_bc = sb("bo_bc", [P, LT, P])
        pr = sb("pr", [STK, 3, FEAT])
        prb = sb("prb", [STK, 3, FEAT], BF16)
        proj_stk = sb("proj_stk", [STK, FEAT], BF16)
        w2_s = sb("w2_s", [P, EXP, HT, P])
        wr_s = sb("wr_s", [P, EXP])
        br_bc = sb("br_bc", [P, EXP])
        iota = sb("iota", [P, EXP])
        base = sb("base", [P, EXP])
        base_0 = sb("base_0", [P, EXP])
        tile_no = sb("tile_no", [P, N_TILES])
        tri = sb("tri", [P, P], F16)
        ones_b = sb("ones_b", [P, P], F16)
        pad_rows = sb("pad_rows", [P, XW])
        rows_s = sb("rows_s", [P, LT, XW])
        lane = sb("lane", [P, 1])
        xr_T = sb("xr_T", [P, LEN])
        lg = sb("lg", [P, LT, EXP])
        top8 = sb("top8", [P, LT, EXP])
        idx8 = sb("idx8", [P, LT, EXP], U32)
        hot = sb("hot", [P, TOPK, LT, EXP])
        picks = sb("picks", [P, LT * EXP], F16)
        slot_m = sb("slot_m", [P, LT, EXP])
        slot_k = sb("slot_k", [P, TOPK, LT, EXP])
        slots = sb("slots", [P, TOPK, LT], U32)
        best = sb("best", [P, TILES, TOPK])
        b1_raw = sb("b1_raw", [EXP * HT, P])
        b1_s = sb("b1_s", [P, EXP * HT])
        nb1 = sb("nb1", [P, EXP * HT])
        b2_s = sb("b2_s", [EXP, P])
        eps_t = sb("eps_t", [P, LT])
        half_t = sb("half_t", [P, LT])
        zero_t = sb("zero_t", [P, LT])
        x_all = sb("x_all", [P, TILES, P])
        x_in = sb("x_in", [P, LT, P])
        xT = sb("xT", [P, LEN])
        qk_f = sb("qk_f", [P, 2, LEN])
        parts = sb("parts", [P, 2, SPL, LEN], BF16)
        stk_mem = sb("stk_mem", [P, 2 * EXP * HID])
        stk = stk_mem[0:STK, :].bitcast(BF16).rearrange("p (s a g n) -> p s a g n", s=2, a=HG, g=G)
        v_pad = sb("v_pad", [P, LT, G, HG * PADW])
        turns = sb("turns", [P, 2, UC], F16)
        feats = sb("feats", [P, HALF, 2, UC])
        kvT = sb("kvT", [P, 2, FEAT])
        c_sum = sb("c_sum", [P, 1])
        kv_c = sb("kv_c", [P, P])
        kv_pad = sb("kv_pad", [P, 2, G, HG * PADW])
        outT = sb("outT", [P, LEN])
        y = sb("y", [P, LT, P])
        stats = sb("stats", [P, LT, 6])
        mv = sb("mv", [P, LT, 2])
        rstd = sb("rstd", [P, LT])
        fflat = feats[:, :, :, :].rearrange("p a b c -> p (a b c)")
        w1_s = stk_mem[:, 0:EXP * HID]
        w1_now = stk_mem[:, EXP * HID:EXP * HID + 2 * HID].rearrange("p (r n) -> p r n", r=2)
        free_at = [0]

        def take(n):
            free_at[0] += n
            return fflat[:, free_at[0] - n:free_at[0]]

        b2_bc = take(EXP * P)
        xg = take(RING_X * XW).rearrange("p (r n) -> p r n", r=RING_X)
        xgT = take(2 * P).rearrange("p (r n) -> p r n", r=2)
        hidT = take(2 * HID).rearrange("p (r n) -> p r n", r=2)
        y_row = take(UNROLL * P).rearrange("p (r n) -> p r n", r=UNROLL)
        first_pick = take(UNROLL).rearrange("p (r n) -> p r n", r=UNROLL)
        spare = take(UNROLL).rearrange("p (r n) -> p r n", r=UNROLL)
        y_at = take(UNROLL).rearrange("p (r n) -> p r n", r=UNROLL).bitcast(U32)
        ended = take(N_TILES * EXP).rearrange("p (i e) -> p i e", i=N_TILES)
        tiles_f = take(4 * EXP).rearrange("p (k e) -> p k e", k=4)
        tab_f = take(6 * N_TILES).rearrange("p (k i) -> p k i", k=6)
        tab_row = take(N_TILES + 1).bitcast(U32)
        tab_e = take(N_TILES + 1).bitcast(U32)
        pad_f = take(EXP)
        pad_at = take(EXP + 1).bitcast(U32)
        gate = take(4 * TILES).rearrange("p (k t) -> p k t", k=4)
        y_back = take(2 * TOPK * LEN).rearrange("p (r k t d) -> p r k t d", r=2, k=TOPK, t=LT)
        y_sum = take(2 * LEN).rearrange("p (r t d) -> p r t d", r=2, t=LT)
        stats_f = take(2 * LT * 6).rearrange("p (r t n) -> p r t n", r=2, t=LT)
        mv_f = take(2 * LT * 2).rearrange("p (r t n) -> p r t n", r=2, t=LT)
        rstd_f = take(2 * LT).rearrange("p (r t) -> p r t", r=2)
        shift_f = take(2 * LT).rearrange("p (r t) -> p r t", r=2)
        y_fin = take(2 * LEN).rearrange("p (r t d) -> p r t d", r=2, t=LT)

        ang = ctx.enter_context(nc.psum_tensor("ang", [P, 3, UC], F32))
        misc = ctx.enter_context(nc.psum_tensor("misc", [P, 2, 512], F32))

        banks = [ang[:, i // 2, (i % 2) * 512:(i % 2) * 512 + 512] for i in range(6)] + \
                [misc[:, i, :] for i in range(2)]
        xT_bank, h_bank, y_bank = banks[0:2], banks[2:4], banks[6:8]

        s = {n: sem(n) for n in (
            "loads", "raw_T", "raw_ev", "pad_ok", "setup", "xin_in", "angles", "rounded", "reduced", "sines",
            "sq_v", "sq_p", "xT_mm", "xT_ev", "q_mm", "q_ev", "k_mm", "k_ev", "v_mm", "v_ev",
            "kvT_mm", "kvT_ev", "kv_mm", "kv_ev", "c_mm", "c_ev", "out_mm", "out_ev", "wo_mm", "y_ok", "bo_ok",
            "ln_stat", "ln_aggr", "ln_eps", "ln_pow", "xn_ok", "split", "parts_out", "moe_in", "xnT_mm", "xnT_ev",
            "lg_mm", "lg_ok", "top_ok", "idx_ok", "hot_ok", "picked", "rk_mm", "slot_ok", "slotk_ok", "slots_ok", "meta", "based",
            "xr_mm", "xr_ev", "x_kept", "scattered", "rt", "b1_mm", "b1_ok", "b2_mm", "b2_ok", "tab_ok", "pads_in",
            "gap_ok", "gap_exp", "gates_ok", "xT_t", "xT_e", "h_t", "h_e", "w1_ok", "y_t", "y_e",
            "pick1", "pick2", "y_at_ok", "sum1", "sum2", "fin_stat", "fin_aggr", "fin_eps", "fin_rstd", "fin_mean", "fin_shift", "fin_ok", "wload", "v_zero", "held",
        )}
        stk_in = [[sem(f"stk_in{side}{g}") for g in range(HG)] for side in range(2)]
        x_in_sem = [sem(f"x_tile_in{r}") for r in range(RING_X)]
        y_sem = [sem(f"y_sent{r}") for r in range(UNROLL)]
        fin_sem = [sem(f"stored{r}") for r in range(2)]
        y_in_sem = [sem(f"y_in{r}") for r in range(2)]
        block = ctx.enter_context(nc.Block())

        def wait(eng, name, per, b, off):
            sm = s[name] if isinstance(name, str) else name
            if isinstance(b, int):
                if per * b + off > 0:
                    eng.wait_ge(sm, per * b + off)
            else:
                eng.wait_ge(sm, b * per + off)

        def hold(eng, name, per, b, off):
            wait(eng, name, per, b, off)
            if not isinstance(b, int):
                eng.sem_inc(s["held"], 1)

        def back(i, r, n):
            return (i, r - n) if r >= n else (i - 1, r - n + UNROLL)

        def dense(pads):
            return pads.rearrange("p n (a w) -> p n a w", a=HG)[:, :, :, 0:DH]

        def tile_steps(eng, steps):
            last = N_TILES // UNROLL
            steps(0, True, False)
            with eng.Fori(1, last - 1) as i:
                steps(i, False, False)
            steps(last - 1, False, False)
            steps(last, False, True)

        def entries(engine, table, i, most, n=UNROLL + 1):
            cols = table[0:1, i * UNROLL:i * UNROLL + n] if isinstance(i, int) \
                else table[0:1, bass.ds(i * UNROLL, n)]
            return nc.values_load_multi_w_load_instructions(cols, engines=[engine], min_val=0, max_val=most)[1]

        def sequences(eng, body):
            body(0, 0)
            with eng.Fori(0, (BATCH - 2) // RING) as i:
                for r in range(RING):
                    body(i * RING + (r + 1), (r + 1) % RING)
            body(BATCH - 1, (BATCH - 1) % RING)

        @block.sync
        def _(sp):
            n = 0
            sp.dma_start(x_in[:, :, :], x_rows[0]).then_inc(s["xin_in"], 16)
            for dst, src in (
                (ident[:, :], c_ident), (w_raw[:, 0, :], Wk), (w_raw[:, 1, :], Wq), (w_raw[:, 2, :], Wv),
                (w_raw[:, 3, :], Wo), (bqk[0:1, :], bk.unsqueeze(0)), (bqk[1:2, :], bq.unsqueeze(0)),
                (negi[:, :], c_negi), (mask[:, :], c_mask),
                (pr[:, 0, :], proj.unsqueeze(0).broadcast_to([SPL * SPL, DH, FEAT])),
                (bv_raw[:, :], bv.partition_broadcast(P)),
                (bo_bc[:, :, :], bo.unsqueeze(0).unsqueeze(0).broadcast_to([P, LT, P])),
            ):
                sp.dma_start(dst, src).then_inc(s["loads"], 16)
                n += 1
            assert n == N_LOADS

            def stack(b):
                def write(side):
                    hold(sp, "split", 6, b, 3 * side + 3)
                    dst = parts_dram[b, side].rearrange("i r n -> r i n")
                    sp.dma_start(dst, parts[:, side, :, :]).then_inc(s["parts_out"], 16)
                    hold(sp, "parts_out", 32, b, 16 * side + 16)

                def read(side, hg):
                    hold(sp, "angles", UNITS, b, HALF * side + 2 * hg + 2 - UNITS)
                    rows = parts_dram[b, side].rearrange("i (d h) n -> (i d) (h n)", d=DH)
                    src = rows[:, hg * G * LEN:(hg + 1) * G * LEN]
                    sp.dma_start(stk[:, side, hg, :, :].rearrange("p g n -> p (g n)"),
                                 src.unsqueeze(0).broadcast_to([SPL, SPL * DH, G * LEN]))\
                        .then_inc(stk_in[side][hg], 16)

                for side in range(2):
                    write(side)
                    for hg in range(HG):
                        read(side, hg)

            def load_x(b):
                hold(sp, "xT_mm", 1, b, 0)
                sp.dma_start(x_in[:, :, :], x_rows[b]).then_inc(s["xin_in"], 16)

            load_x(1)
            stack(0)
            for t in range(BATCH):
                sp.dma_start(x_all[:, t * LT:(t + 1) * LT, :], x_rows[t]).then_inc(s["wload"], 16)
            sp.dma_start(w2_s[:, :, :, :], W2.rearrange("e (j p) d -> p e j d", p=P)).then_inc(s["wload"], 16)
            sp.dma_start(wr_s[:, :], Wr).then_inc(s["wload"], 16)
            sp.dma_start(br_bc[:, :], br.partition_broadcast(P)).then_inc(s["wload"], 16)
            for dst, src in ((iota[:, :], c_iota.partition_broadcast(P)), (base[:, :], c_base.partition_broadcast(P)),
                             (base_0[:, :], c_base.partition_broadcast(P)), (tile_no[:, :], c_tile.partition_broadcast(P)),
                             (tri[:, :], c_tri), (pad_rows[:, :], c_pad)):
                sp.dma_start(dst, src).then_inc(s["wload"], 16)
            sp.dma_start(rows_s[:, :, P:XW], c_tok).then_inc(s["wload"], 16)
            sp.dma_start(b1_raw[:, :], b1.rearrange("e (j p) -> (e j) p", p=P)).then_inc(s["wload"], 16)
            sp.dma_start(b2_s[:, :], b2).then_inc(s["wload"], 16)
            with sp.Fori(1, BATCH - 1) as b:
                load_x(b + 1)
                stack(b)
            stack(BATCH - 1)
            sp.wait_ge(s["angles"], UNITS * BATCH)
            sp.dma_start(w1_s.rearrange("p (e h) -> p e h", e=EXP), W1.rearrange("e d h -> d e h"))\
                .then_inc(s["moe_in"], 16)
            sp.wait_ge(s["tab_ok"], 2)
            sp.wait_ge(s["scattered"], 16 * TOPK * TILES)
            sp.wait_ge(s["pads_in"], 16 * (EXP + 1))

            def load_tile(i, r, q, row):
                if q >= 0:
                    hold(sp, "xT_t", UNROLL, i, r + 1 - RING_X)
                    hold(sp, "y_at_ok", UNROLL, i, r + 1 - RING_X)
                sp.dma_start(xg[:, r, :], routed_dram[bass.ds(row, P), :]).then_inc(x_in_sem[r], 16)

            rows = entries(mybir.EngineType.SP, tab_row, 0, (EXP + 1) * REGION - P)
            for r in range(UNROLL):
                load_tile(0, r, -1, rows[r + 1])
            with sp.Fori(1, N_TILES // UNROLL) as i:
                rows = entries(mybir.EngineType.SP, tab_row, i, (EXP + 1) * REGION - P)
                for r in range(UNROLL):
                    load_tile(i, r, 0, rows[r + 1])
            for r in range(UNROLL):
                sp.wait_ge(y_sem[r], 16 * N_TILES // UNROLL)
            back = expert_dram[0:TOPK * ROWS, :].rearrange("(k b t p) d -> b k p t d", k=TOPK, t=LT, p=P)

            def bring(b, r):
                if not isinstance(b, int):
                    hold(sp, "sum2", 2, b, r - 1)
                for k in range(TOPK):
                    sp.dma_start(y_back[:, r, k, :, :], back[b * 2 + r, k]).then_inc(y_in_sem[r], 16)

            def store(b, r):
                hold(sp, "fin_ok", 2, b, r + 1)
                sp.dma_start(out_rows[b * 2 + r], y_fin[:, r, :, :]).then_inc(fin_sem[r], 16)

            bring(0, 0)
            bring(0, 1)
            with sp.Fori(1, BATCH // 2) as b:
                for r in range(2):
                    bring(b, r)
                    store(b - 1, r)
            for r in range(2):
                store(BATCH // 2 - 1, r)
            for r in range(2):
                sp.wait_ge(fin_sem[r], 16 * BATCH // 2)

        @block.tensor
        def _(pe):
            pe.wait_ge(s["loads"], 16 * N_LOADS)
            for i in range(3):
                mm = pe.transpose(misc[:, 0, i * P:(i + 1) * P], w_raw[:, i, :], ident[:, :])
            pe.wait_ge(s["pad_ok"], 2)
            mm = pe.transpose(misc[:, 0, 3 * P:3 * P + 2], bqk_p[:, :], ident[0:2, 0:2])
            mm.then_inc(s["raw_T"], 1)
            pe.transpose(misc[:, 1, 0:P], wo_perm[:, :], ident[:, :]).then_inc(s["raw_T"], 1)

            def x_T(b, *free):
                wait(pe, "xin_in", 16, b, 16)
                wait(pe, *free)
                for t in range(LT):
                    mm = pe.transpose(misc[:, 0, t * P:(t + 1) * P], x_in[:, t, :], ident[:, :])
                mm.then_inc(s["xT_mm"], 1)

            def project(side, bank, b, *free):
                wait(pe, "xT_ev", 1, b, 1)
                wait(pe, *free)
                pe.matmul(misc[:, bank, :], wT[:, side, :], xT[:, :], start=True, stop=True)\
                    .then_inc(s["kq"[side] + "_mm"], 1)

            def v_product(b, bank, *free):
                wait(pe, *free)
                for t in range(LT):
                    mm = pe.matmul(misc[:, bank, t * P:(t + 1) * P], xT[:, t * P:(t + 1) * P], wT[:, 2, :],
                                   start=True, stop=True)
                mm.then_inc(s["v_mm"], 1)

            x_T(0, "raw_ev", 0, 0, 2)
            project(0, 1, 0, "raw_ev", 0, 0, 2)
            project(1, 0, 0, "xT_ev", 0, 0, 1)
            v_product(0, 1, "k_ev", 0, 0, 1)

            def angles(b, ph, u):
                side, hg, half = u // HALF, u % HALF // 2, u % 2
                if half == 0:
                    wait(pe, stk_in[side][hg], 16, b, 16)
                wait(pe, "sines", UNITS, b, u - RING + 1)
                a = ang[:, slot(ph, u), :]
                if side == 0:
                    for t in range(2):
                        for g in range(G):
                            at = (t * G + g) * FEAT
                            tok = (2 * half + t) * P
                            mm = pe.matmul(a[:, at:at + FEAT], stk[:, 0, hg, g, tok:tok + P], proj_stk[:, :],
                                           start=(g == 0), stop=False, skip_group_check=True)
                else:
                    for t in range(2):
                        mm = pe.matmul(a[:, t * 512:(t + 1) * 512], proj_stk[:, :],
                                       stk[:, 1, hg, 2 * half + t, :], start=True, stop=False,
                                       skip_group_check=True)
                mm.then_inc(s["angles"], 1)

            def reduce_turns(b, ph, u):
                wait(pe, "rounded", UNITS, b, u + 1)
                for t in range(2):
                    mm = pe.matmul(ang[:, slot(ph, u), t * 512:(t + 1) * 512], negi[:, :],
                                   turns[:, u % 2, t * 512:(t + 1) * 512], start=False, stop=True,
                                   skip_group_check=True)
                mm.then_inc(s["reduced"], 1)

            def squared(b, u):
                wait(pe, "sq_v", UNITS - len(POOL_SQ), b, before(u + 1, False))
                wait(pe, "sq_p", len(POOL_SQ), b, before(u + 1, True))

            def kv_product(b, u, *free):
                hg, half = u // 2, u % 2
                squared(b, u)
                if u == 0:
                    wait(pe, "v_ev", 1, b, 1)
                    wait(pe, *free)
                for t in range(2):
                    for g in range(G):
                        at = (t * G + g) * FEAT
                        mm = pe.matmul(misc[32 * g:32 * g + 32, 0, 0:2 * FEAT].rearrange("p (a m) -> p a m", a=2),
                                       v_pad[:, 2 * half + t, g, hg * PADH:(hg + 1) * PADH],
                                       feats[:, u, :, at:at + FEAT],
                                       start=(u == 0 and t == 0), stop=(u == HALF - 1 and t == 1),
                                       skip_group_check=True)
                mm.then_inc(s["kvT_mm"], 1)

            def kv_turn(b):
                wait(pe, "kvT_ev", 1, b, 1)
                o = misc[:, 0, :]
                pe.matmul(o[:, 0:P], kvT[:, 0, :], ident[:, :], start=True, stop=True, skip_group_check=True)
                pe.matmul(o[:, P:2 * P], kvT[:, 1, :], ident4[:, :], start=True, stop=False, skip_group_check=True)
                for t in range(LT):
                    mm = pe.matmul(o[:, P:2 * P], minus_2[:, :], dense(v_pad[:, t, :, :]),
                                   start=False, stop=(t == LT - 1), skip_group_check=True)
                mm.then_inc(s["kv_mm"], 1)

            def c_product(b):
                wait(pe, "kv_ev", 1, b, 1)
                pe.matmul(misc[:, 0, 2 * P:2 * P + 2], kv_c[:, :], minus_half[:, :], start=True, stop=True)\
                    .then_inc(s["c_mm"], 1)

            def out_product(b, hg, a, *free):
                u = HALF + 2 * hg
                if a == 0:
                    wait(pe, "sines", UNITS, b, u + 2)
                else:
                    squared(b, u + 1)
                if hg == 0 and a == 0:
                    wait(pe, "kv_ev", 1, b, 1)
                    wait(pe, *free)
                for g in range(G):
                    mm = pe.matmul(misc[32 * g:32 * g + 32, 1, :], kv_pad[:, a, g, hg * PADH:(hg + 1) * PADH],
                                   feats[:, 2 * hg + g // 2, a, (g % 2) * LEN:(g % 2 + 1) * LEN],
                                   start=(hg == 0 and a == 0), stop=(hg == HG - 1 and a == 1),
                                   skip_group_check=True)
                if a == 1:
                    mm.then_inc(s["out_mm"], 1)

            def wo_product(b):
                wait(pe, "out_ev", 1, b, 1)
                for t in range(LT):
                    mm = pe.matmul(misc[:, 1, t * P:(t + 1) * P], outT[:, t * P:(t + 1) * P], woT[:, :],
                                   start=True, stop=True)
                mm.then_inc(s["wo_mm"], 1)

            def rows_T(b, *free):
                wait(pe, "xn_ok", 1, b, 1)
                wait(pe, *free)
                for t in range(LT):
                    mm = pe.transpose(misc[:, 1, t * P:(t + 1) * P], rows_s[:, t, 0:P], ident[:, :])
                mm.then_inc(s["xr_mm"], 1)

            def logits(b, *free):
                wait(pe, "xr_ev", 1, b, 1)
                wait(pe, *free)
                for t in range(LT):
                    mm = pe.matmul(misc[:, 1, t * EXP:(t + 1) * EXP], xr_T[:, t * P:(t + 1) * P], wr_s[:, :],
                                   start=True, stop=True)
                mm.then_inc(s["lg_mm"], 1)

            def ranks(b, *free):
                wait(pe, "picked", 1, b, 1)
                wait(pe, *free)
                o = misc[:, 1, :]
                n = LT * EXP
                pe.matmul(o[:, 0:n], tri[:, :], picks[:, :], start=True, stop=False, skip_group_check=True)
                for t in range(1, LT):
                    pe.matmul(o[:, t * EXP:n], ones_b[:, :], picks[:, 0:n - t * EXP],
                              start=False, stop=False, skip_group_check=True)
                for t in range(LT):
                    mm = pe.matmul(o[:, n:n + EXP], ones_b[:, :], picks[:, t * EXP:(t + 1) * EXP],
                                   start=False, stop=(t == LT - 1), skip_group_check=True)
                mm.then_inc(s["rk_mm"], 1)

            def body(b, ph):
                first = isinstance(b, int) and b == 0
                last = isinstance(b, int) and b == BATCH - 1
                for u in range(UNITS):
                    angles(b, ph, u)
                    if not (first and u == 0):
                        reduce_turns(b, ph, u - 1)
                    if u == 0 and not first:
                        out_product(b - 1, 2, 0)
                        out_product(b - 1, 2, 1)
                    if u == 1:
                        if not last:
                            x_T(b + 1, *(("q_ev", 1, b, 1) if first else ("v_ev", 1, b, 1)))
                        if not first:
                            out_product(b - 1, 3, 0)
                    if u == 2 and not first:
                        out_product(b - 1, 3, 1)
                    if u in KV_STEP:
                        kv_product(b, KV_STEP.index(u), *(("v_ev", 1, b, 1) if last else ("xT_ev", 1, b, 2)))
                    if u == 4 and not first:
                        wo_product(b - 1)
                    if u == 6 and not last:
                        project(0, 1, b + 1, *(("v_ev", 1, b, 1) if first else ("y_ok", 1, b, 0)))
                    if u == 7 and not last:
                        project(1, 1, b + 1, "k_ev", 1, b, 2)
                    if u == 8 and not first:
                        rows_T(b - 1, *(("y_ok", 1, b, 0) if last else ("q_ev", 1, b, 2)))
                    if u == 9 and not first:
                        logits(b - 1, "xr_ev", 1, b, 0)
                    if u == 12:
                        kv_turn(b)
                        if not first:
                            ranks(b - 1, "lg_ok", 1, b, 0)
                    if u == 13:
                        out_product(b, 0, 0, *(("q_ev", 1, b, 2) if first else ("based", 1, b, 0)))
                        out_product(b, 0, 1)
                    if u == 14:
                        c_product(b)
                        out_product(b, 1, 0)
                    if u == 15:
                        out_product(b, 1, 1)
                        if not last:
                            v_product(b + 1, 0, "c_ev", 1, b, 1)

            pe.wait_ge(s["setup"], N_SETUP)
            sequences(pe, body)
            e = BATCH
            reduce_turns(e, e % RING, -1)
            for hg in (2, 3):
                for a in range(2):
                    out_product(e - 1, hg, a)
            wo_product(e - 1)
            rows_T(e - 1, "y_ok", 1, e, 0)
            logits(e - 1, "xr_ev", 1, e, 0)
            ranks(e - 1, "lg_ok", 1, e, 0)

            pe.transpose(y_bank[0][:, 0:EXP * HT], b1_raw[:, :], ident[0:EXP * HT, 0:EXP * HT])\
                .then_inc(s["b1_mm"], 1)
            pe.wait_ge(s["sines"], UNITS * BATCH)
            pe.wait_ge(s["b1_ok"], 1)
            for x_e in range(EXP):
                o = banks[x_e // 4][:, (x_e % 4) * P:(x_e % 4 + 1) * P]
                pe.matmul(o, ident[0:EXP, x_e:x_e + 1].broadcast_to([EXP, P]), b2_s[:, :], start=True, stop=False)
                for j in range(HT):
                    mm = pe.matmul(o, b1_s[:, x_e * HT + j:x_e * HT + j + 1].broadcast_to([P, P]), w2_s[:, x_e, j, :],
                                   start=False, stop=(j == HT - 1))
            mm.then_inc(s["b2_mm"], 1)
            pe.wait_ge(s["b2_ok"], 1)
            pe.wait_ge(s["tab_ok"], 2)
            pe.wait_ge(s["based"], BATCH)

            def x_turn(i, r):
                wait(pe, x_in_sem[r % RING_X], 16, i, 16 * (r // RING_X) + 16)
                wait(pe, "xT_e", UNROLL, i, r - 1)
                pe.transpose(xT_bank[r % 2][:, 0:P], xg[:, r % RING_X, 0:P], ident[:, :]).then_inc(s["xT_t"], 1)

            def first_layer(i, r):
                wait(pe, "xT_e", UNROLL, i, r + 1)
                wait(pe, "w1_ok", UNROLL, i, r + 1)
                wait(pe, "h_e", UNROLL, i, r - 1)
                for j in range(HT):
                    mm = pe.matmul(h_bank[r % 2][:, j * P:(j + 1) * P], w1_now[:, r % 2, j * P:(j + 1) * P],
                                   xgT[:, r % 2, :], start=True, stop=True)
                mm.then_inc(s["h_t"], 1)

            def second_layer(i, r, x_e):
                wait(pe, "h_e", UNROLL, i, r + 1)
                wait(pe, "y_e", UNROLL, i, r - 1)
                w2_e = w2_s[:, bass.ds(x_e, 1), :, :].rearrange("p a j d -> p (a j) d")
                for j in range(HT):
                    mm = pe.matmul(y_bank[r % 2][:, 0:P], hidT[:, r % 2, j * P:(j + 1) * P],
                                   w2_e[:, j, :], start=(j == 0), stop=(j == HT - 1))
                mm.then_inc(s["y_t"], 1)

            def steps(i, head, tail):
                x_e = entries(mybir.EngineType.PE, tab_e, i, EXP - 1, 1 if tail else UNROLL + 1)
                for r in range(UNROLL):
                    if not tail:
                        first_layer(i, r)
                    if not (head and r < 1) and not (tail and r > 0):
                        second_layer(*back(i, r, 1), x_e[r])
                    if not tail and not (r >= UNROLL - 2 and isinstance(i, int)
                                         and i == N_TILES // UNROLL - 1):
                        x_turn(i, r + 2)

            x_turn(0, 0)
            x_turn(0, 1)
            tile_steps(pe, steps)

        @block.scalar
        def _(act):
            def out_evac(b):
                wait(act, "out_mm", HG, b, HG)
                wait(act, "c_ev", 1, b, 1)
                wait(act, "wo_mm", 1, b, 0)
                act.activation(outT[:, :], misc[:, 1, :], ACT.Identity, bias=c_sum[:, :]).then_inc(s["out_ev"], 1)

            def proj_evac(b, side, bank):
                wait(act, "kq"[side] + "_mm", 1, b, 1)
                wait(act, "split", 6, b, 3 * side - 3)
                wait(act, "parts_out", 32, b, 16 * side - 16)
                act.activation(parts[:, side, 0, :], misc[:, bank, :], ACT.Identity,
                               bias=bqk_t[:, side:side + 1], scale=TURN)
                act.activation(qk_f[:, side, :], misc[:, bank, :], ACT.Identity,
                               bias=bqk_t[:, side:side + 1], scale=TURN).then_inc(s["kq"[side] + "_ev"], 1)

            def sines(b, ph, u):
                wait(act, "reduced", UNITS, b, u + 1)
                if u < HALF:
                    wait(act, "out_mm", HG, b, u // 2 + 1 - HG)
                else:
                    wait(act, "kvT_mm", HALF, b, u - HALF + 1)
                a = ang[:, slot(ph, u), :]
                f = feats[:, u % HALF, :, :]
                act.activation(f[:, 0, :], a, ACT.Sin, scale=TWO_PI)
                act.activation(f[:, 1, :], a, ACT.Sin, scale=TWO_PI / 2).then_inc(s["sines"], 1)

            def rows_evac(b):
                wait(act, "xr_mm", 1, b, 1)
                act.activation(xr_T[:, :], misc[:, 1, :], ACT.Copy).then_inc(s["xr_ev"], 1)

            def keep_rows(b):
                wait(act, "xn_ok", 1, b, 1)
                xb = x_all[:, b * LT:(b + 1) * LT, :] if isinstance(b, int) else x_all[:, bass.ds(b * LT, LT), :]
                act.activation(xb, rows_s[:, :, 0:P], ACT.Copy).then_inc(s["x_kept"], 1)

            act.wait_ge(s["setup"], 1)
            proj_evac(0, 0, 1)
            proj_evac(0, 1, 0)

            def body(b, ph):
                first = isinstance(b, int) and b == 0
                last = isinstance(b, int) and b == BATCH - 1
                for u in range(UNITS):
                    if u == 3 and not first:
                        out_evac(b - 1)
                    if u in (6, 7) and not last:
                        proj_evac(b + 1, u - 6, 1)
                    if u == 8 and not first:
                        rows_evac(b - 1)
                    if u == 10 and not first:
                        keep_rows(b - 1)
                    sines(b, ph, u)

            sequences(act, body)
            out_evac(BATCH - 1)

            rows_evac(BATCH - 1)
            keep_rows(BATCH - 1)
            act.wait_ge(s["gap_ok"], 1)
            act.activation(gate[:, 1, :], gate[:, 0, :], ACT.Exp).then_inc(s["gap_exp"], 1)
            act.wait_ge(s["moe_in"], 16)
            act.wait_ge(s["tab_ok"], 2)

            def weights(i, r, x_e):
                wait(act, "h_t", UNROLL, i, r - 1)
                act.activation(w1_now[:, r % 2, :], w1_s[:, bass.ds(x_e * HID, HID)], ACT.Copy)\
                    .then_inc(s["w1_ok"], 1)

            def steps(i, head, tail):
                if not tail:
                    x_e = entries(mybir.EngineType.Activation, tab_e, i, EXP - 1)
                    for r in range(UNROLL):
                        weights(i, r, x_e[r + 1])

            tile_steps(act, steps)

            def final_norm(b, r):
                wait(act, "fin_shift", 2, b, r + 1)
                wait(act, fin_sem[r], 16, b, 0)
                for t in range(LT):
                    ins = act.activation(y_fin[:, r, t, :], y_sum[:, r, t, :], ACT.Identity,
                                         bias=shift_f[:, r, t:t + 1], scale=rstd_f[:, r, t:t + 1])
                ins.then_inc(s["fin_ok"], 1)

            for r in range(2):
                final_norm(0, r)
            with act.Fori(1, BATCH // 2) as b:
                for r in range(2):
                    final_norm(b, r)

        @block.vector
        def _(dve):
            dve.memset(minus_2[:, :], -2.0)
            dve.memset(minus_half[:, :], -0.5)
            dve.memset(eps_t[:, :], EPS)
            dve.memset(ones_b[:, :], 1.0)
            dve.memset(half_t[:, :], -0.5)
            dve.memset(zero_t[:, :], 0.0)
            dve.wait_ge(s["loads"], 16 * N_LOADS)
            dve.tensor_scalar(ident4[:, :], ident[:, :], 4.0, None, ALU.mult)
            dve.tensor_copy(wo_perm[:, :].rearrange("p (g a d) -> p g a d", a=HG, g=G),
                            w_raw[:, 3, :].rearrange("p (a g d) -> p g a d", a=HG, g=G)).then_inc(s["pad_ok"], 1)
            dve.tensor_copy(bqk_p[:, :].rearrange("p (d h) -> p d h", d=DH),
                            bqk[:, :].rearrange("p (h d) -> p d h", d=DH)).then_inc(s["pad_ok"], 1)
            for t in range(LT):
                dve.tensor_scalar(bv_bc[:, t, :].rearrange("p (g a d) -> p g a d", a=HG, g=G),
                                  bv_raw[:, :].rearrange("p (a g d) -> p g a d", a=HG, g=G), KV_SCALE, None,
                                  ALU.mult)
            dve.wait_ge(s["raw_T"], 1)
            for a in range(2):
                dve.tensor_copy(wT[:, a, :].rearrange("p (d h) -> p d h", d=DH),
                                misc[:, 0, a * P:(a + 1) * P].rearrange("p (h d) -> p d h", d=DH))
            dve.tensor_scalar(bqk_t[:, :], misc[:, 0, 3 * P:3 * P + 2], TURN, None, ALU.mult).then_inc(s["setup"], 1)
            dve.tensor_copy(wT[:, 2, :].rearrange("p (g a d) -> p g a d", a=HG, g=G),
                            misc[:, 0, 2 * P:3 * P].rearrange("p (a g d) -> p g a d", a=HG, g=G))\
                .then_inc(s["raw_ev"], 1)
            dve.wait_ge(s["raw_T"], 2)
            dve.tensor_copy(woT[:, :], misc[:, 1, 0:P]).then_inc(s["raw_ev"], 1)
            n_set = [1]

            def chain(ins):
                n_set[0] += 1
                ins.then_inc(s["setup"], 1)
                dve.wait_ge(s["setup"], n_set[0])

            def x_evac(b):
                wait(dve, "xT_mm", 1, b, 1)
                dve.tensor_copy(xT[:, :], misc[:, 0, :]).then_inc(s["xT_ev"], 1)

            x_evac(0)
            for i in range(SPL):
                chain(dve.tensor_copy(prb[:, i, :], pr[:, i, :]))
                if i < SPL - 1:
                    chain(dve.tensor_tensor(pr[:, i + 1, :], pr[:, i, :], prb[:, i, :], ALU.subtract))
            chain(dve.tensor_scalar(pr[:, 0, :], prb[:, 0, :], mask[:, 0:1], None, ALU.mult))
            chain(dve.scalar_tensor_tensor(out=pr[:, 1, :], in0=prb[:, 1, :], scalar=mask[:, 1:2],
                                           in1=pr[:, 0, :], op0=ALU.mult, op1=ALU.add))
            chain(dve.scalar_tensor_tensor(out=proj_stk[:, :], in0=prb[:, 2, :], scalar=mask[:, 2:3],
                                           in1=pr[:, 1, :], op0=ALU.mult, op1=ALU.add))
            assert n_set[0] == N_SETUP

            def round_turns(b, ph, u):
                wait(dve, "angles", UNITS, b, u + 1)
                wait(dve, "reduced", UNITS, b, u - 1)
                dve.tensor_scalar(turns[:, u % 2, :], ang[:, slot(ph, u), :], MAGIC, -MAGIC, ALU.add, ALU.add)\
                    .then_inc(s["rounded"], 1)

            def square(b, u):
                if u % UNITS in POOL_SQ:
                    return
                wait(dve, "sines", UNITS, b, u + 1)
                f = feats[:, u % HALF, 1, :]
                dve.tensor_tensor(f, f, f, ALU.mult).then_inc(s["sq_v"], 1)

            def kvT_evac(b):
                wait(dve, "kvT_mm", HALF, b, HALF)
                dve.tensor_copy(kvT[:, :, :].rearrange("p a m -> p (a m)"), misc[:, 0, 0:2 * P])\
                    .then_inc(s["kvT_ev"], 1)

            def kv_evac(b):
                wait(dve, "kv_mm", 1, b, 1)
                wait(dve, "out_mm", HG, b, 0)
                dve.tensor_copy(kv_c[:, :], misc[:, 0, P:2 * P])
                dve.tensor_copy(dense(kv_pad[:, :, :, :].rearrange("p a g w -> p (a g) w")),
                                misc[:, 0, 0:2 * P].rearrange("p (g a d) -> p g a d", a=HG, d=DH))\
                    .then_inc(s["kv_ev"], 1)

            def c_evac(b):
                wait(dve, "c_mm", 1, b, 1)
                wait(dve, "out_ev", 1, b, 0)
                dve.tensor_copy(c_sum[:, :], misc[:, 0, 2 * P:2 * P + 1]).then_inc(s["c_ev"], 1)

            def v_evac(b, bank):
                wait(dve, "v_mm", 1, b, 1)
                dve.scalar_tensor_tensor(out=dense(v_pad[:, :, :, :].rearrange("p t g w -> p (t g) w")),
                                         in0=misc[:, bank, :].rearrange("p (g a d) -> p g a d", a=HG, d=DH),
                                         scalar=KV_SCALE,
                                         in1=bv_bc[:, :, :].rearrange("p t (g a d) -> p (t g) a d", a=HG, d=DH),
                                         op0=ALU.mult, op1=ALU.add).then_inc(s["v_ev"], 1)

            def statistics(b):
                wait(dve, "y_ok", 1, b, 1)
                for t in range(LT):
                    ins = dve.bn_stats(stats[:, t, :], y[:, t, :])
                ins.then_inc(s["ln_stat"], 1)

            def moments(b):
                hold(dve, "ln_stat", 1, b, 1)
                for t in range(LT):
                    ins = dve.bn_aggr(mv[:, t, :], stats[:, t, :])
                ins.then_inc(s["ln_aggr"], 1)

            def normalize(b):
                wait(dve, "ln_pow", 1, b, 1)
                wait(dve, "scattered", 16 * TOPK * LT, b, 0)
                wait(dve, "x_kept", 1, b, 0)
                for t in range(LT):
                    ins = dve.tensor_scalar(rows_s[:, t, 0:P], y[:, t, :], mv[:, t, 0:1], rstd[:, t:t + 1],
                                            ALU.subtract, ALU.mult)
                ins.then_inc(s["xn_ok"], 1)

            def over(v, shape):
                return v.broadcast_to(shape)

            tile8 = [P, LT, EXP]

            def take_logits(b):
                wait(dve, "lg_mm", 1, b, 1)
                dve.tensor_tensor(lg[:, :, :], misc[:, 1, 0:LT * EXP].rearrange("p (t e) -> p t e", e=EXP),
                                  over(br_bc[:, :].unsqueeze(1), tile8), ALU.add).then_inc(s["lg_ok"], 1)

            def largest(b):
                hold(dve, "lg_ok", 1, b, 1)
                for t in range(LT):
                    ins = dve.max(top8[:, t, :], lg[:, t, :])
                ins.then_inc(s["top_ok"], 1)

            def which(b):
                hold(dve, "top_ok", 1, b, 1)
                for t in range(LT):
                    ins = dve.max_index(idx8[:, t, :], top8[:, t, :], lg[:, t, :])
                ins.then_inc(s["idx_ok"], 1)

            def chosen(b):
                wait(dve, "idx_ok", 1, b, 1)
                for k in range(TOPK):
                    ins = dve.tensor_tensor(hot[:, k, :, :], over(iota[:, :].unsqueeze(1), tile8),
                                            over(idx8[:, :, k:k + 1], tile8), ALU.is_equal)
                ins.then_inc(s["hot_ok"], 1)

            def pick_both(b):
                wait(dve, "hot_ok", 1, b, 1)
                dve.tensor_tensor(picks[:, :], hot[:, 0, :, :].rearrange("p t e -> p (t e)"),
                                  hot[:, 1, :, :].rearrange("p t e -> p (t e)"), ALU.add).then_inc(s["picked"], 1)
                bb = best[:, b * LT:(b + 1) * LT, :] if isinstance(b, int) else best[:, bass.ds(b * LT, LT), :]
                dve.tensor_copy(bb, top8[:, :, 0:TOPK])
                dve.tensor_copy(rows_s[:, :, P:P + 1], idx8[:, :, 0:1])
                dve.tensor_scalar(rows_s[:, :, P + 1:XW], rows_s[:, :, P + 1:XW], float(LEN), None, ALU.add)\
                    .then_inc(s["meta"], 1)

            n_picks = LT * EXP

            def take_ranks(b):
                wait(dve, "rk_mm", 1, b, 1)
                wait(dve, "based", 1, b, 0)
                dve.tensor_tensor(slot_m[:, :, :], misc[:, 1, 0:n_picks].rearrange("p (t e) -> p t e", e=EXP),
                                  over(base[:, :].unsqueeze(1), tile8), ALU.add).then_inc(s["slot_ok"], 1)

            def slots_of_picks(b):
                wait(dve, "slot_ok", 1, b, 1)
                dve.tensor_tensor(base[:, :], misc[:, 1, n_picks:n_picks + EXP], base[:, :], ALU.add)\
                    .then_inc(s["based"], 1)
                for k in range(TOPK):
                    ins = dve.tensor_tensor(slot_k[:, k, :, :], hot[:, k, :, :], slot_m[:, :, :], ALU.mult)
                ins.then_inc(s["slotk_ok"], 1)

            def slot_numbers(b):
                wait(dve, "slotk_ok", 1, b, 1)
                with nc.allow_low_precision(reason="one whole number among zeros, kept exactly"):
                    dve.tensor_reduce(slots[:, :, :], slot_k[:, :, :, :], AX.X, ALU.add).then_inc(s["slots_ok"], 1)

            def residual(b):
                wait(dve, "wo_mm", 1, b, 1)
                dve.wait_ge(s["bo_ok"], BATCH)
                dve.wait_ge(s["wload"], 16 * N_WLOADS)
                xb = x_all[:, b * LT:(b + 1) * LT, :] if isinstance(b, int) else x_all[:, bass.ds(b * LT, LT), :]
                dve.tensor_tensor(y[:, :, :], misc[:, 1, :].rearrange("p (t d) -> p t d", t=LT), xb, ALU.add)\
                    .then_inc(s["y_ok"], 1)

            dve.wait_ge(s["v_zero"], 2)
            v_evac(0, 1)

            BEFORE_ROUND = ((6, moments), (10, take_logits), (11, chosen), (13, slots_of_picks))
            AFTER_ROUND = ((5, residual), (10, largest), (13, slot_numbers))
            AFTER_SQUARE = ((5, statistics), (7, normalize), (10, which), (11, pick_both), (12, take_ranks))

            def body(b, ph):
                first = isinstance(b, int) and b == 0
                last = isinstance(b, int) and b == BATCH - 1
                for u in range(UNITS):
                    for step, piece in (() if first else BEFORE_ROUND):
                        if u == step:
                            piece(b - 1)
                    round_turns(b, ph, u)
                    if u == 11:
                        kvT_evac(b)
                    for step, piece in (() if first else AFTER_ROUND):
                        if u == step:
                            piece(b - 1)
                    if u == 14:
                        c_evac(b)
                    if not (first and u < 2):
                        square(b, u - 2)
                    for step, piece in (() if first else AFTER_SQUARE):
                        if u == step:
                            piece(b - 1)
                    if u == 1 and not last:
                        x_evac(b + 1)
                    if u == 12:
                        kv_evac(b)
                    if u == 15 and not last:
                        v_evac(b + 1, 0)

            sequences(dve, body)
            e = BATCH
            square(e, -2)
            square(e, -1)
            for piece in (residual, statistics, moments, normalize, take_logits, largest, which, chosen, pick_both,
                          take_ranks, slots_of_picks, slot_numbers):
                piece(e - 1)

            n_rt = [0]

            def rchain(ins):
                n_rt[0] += 1
                ins.then_inc(s["rt"], 1)
                dve.wait_ge(s["rt"], n_rt[0])

            dve.wait_ge(s["based"], BATCH)
            dve.wait_ge(s["out_ev"], BATCH)
            cnt, full, cum_a, cum_b = (tiles_f[:, k, :] for k in range(4))
            rchain(dve.tensor_scalar(lane[:, :], pad_rows[:, P + 1:XW], -float(TOPK * ROWS), None, ALU.add))
            rchain(dve.tensor_scalar(pad_f, base[:, :], lane[:, 0:1], None, ALU.add))
            dve.tensor_copy(pad_at[:, 0:EXP], pad_f)
            rchain(dve.tensor_scalar(pad_at[:, EXP:EXP + 1], lane[:, :], float(EXP * REGION), None, ALU.add))
            rchain(dve.tensor_tensor(cnt, base[:, :], base_0[:, :], ALU.subtract))
            rchain(dve.tensor_scalar(cnt, cnt, 1.0 / P, MAGIC_LAST, ALU.mult, ALU.add))
            rchain(dve.tensor_scalar(full, cnt, MAGIC, -MAGIC, ALU.add, ALU.add))
            src, dst = full, cum_a
            for d in (1, 2, 4):
                dve.tensor_copy(dst[:, 0:d], src[:, 0:d])
                rchain(dve.tensor_tensor(dst[:, d:EXP], src[:, d:EXP], src[:, 0:EXP - d], ALU.add))
                src, dst = dst, (cum_b if dst is cum_a else cum_a)
            cube = [P, N_TILES, EXP]
            rchain(dve.tensor_tensor(ended, over(tile_no[:, :].unsqueeze(2), cube), over(src.unsqueeze(1), cube),
                                     ALU.is_ge))
            e_f, start_f, in_use, e_w, row_f, spare_f = (tab_f[:, k, :] for k in range(6))
            rchain(dve.tensor_scalar(spare_f, tile_no[:, :], float(P), None, ALU.mult))
            rchain(dve.tensor_reduce(e_f, ended, AX.X, ALU.add))
            rchain(dve.tensor_tensor(ended, ended, over(full.unsqueeze(1), cube), ALU.mult))
            rchain(dve.tensor_reduce(start_f, ended, AX.X, ALU.add))
            rchain(dve.tensor_tensor(start_f, tile_no[:, :], start_f, ALU.subtract))
            rchain(dve.tensor_scalar(in_use, e_f, float(EXP), float(P), ALU.is_lt, ALU.mult))
            rchain(dve.tensor_tensor(start_f, start_f, in_use, ALU.mult))
            rchain(dve.scalar_tensor_tensor(out=row_f, in0=e_f, scalar=float(REGION), in1=start_f,
                                            op0=ALU.mult, op1=ALU.add))
            rchain(dve.tensor_scalar(e_w, e_f, float(EXP - 1), None, ALU.min))
            dve.memset(tab_row[:, 0:1], 0)
            dve.memset(tab_e[:, 0:1], 0)
            dve.tensor_copy(tab_row[:, 1:], row_f).then_inc(s["tab_ok"], 1)
            dve.tensor_copy(tab_e[:, 1:], e_w).then_inc(s["tab_ok"], 1)
            dve.tensor_tensor(gate[:, 0, :], best[:, :, 1], best[:, :, 0], ALU.subtract).then_inc(s["gap_ok"], 1)
            dve.wait_ge(s["b1_mm"], 1)
            dve.tensor_copy(b1_s[:, :], y_bank[0][:, 0:EXP * HT])
            dve.tensor_scalar(nb1[:, :], y_bank[0][:, 0:EXP * HT], -1.0, None, ALU.mult).then_inc(s["b1_ok"], 1)
            dve.wait_ge(s["b2_mm"], 1)
            dve.tensor_copy(b2_bc[:, 0:512], banks[0])
            dve.tensor_copy(b2_bc[:, 512:1024], banks[1]).then_inc(s["b2_ok"], 1)
            dve.wait_ge(s["gap_exp"], 1)
            rchain(dve.tensor_scalar(gate[:, 2, :], gate[:, 1, :], 1.0, None, ALU.add))
            rchain(dve.reciprocal(gate[:, 2, :], gate[:, 2, :]))
            dve.tensor_tensor(gate[:, 3, :], gate[:, 1, :], gate[:, 2, :], ALU.mult).then_inc(s["gates_ok"], 1)
            dve.wait_ge(s["b1_ok"], 1)
            dve.wait_ge(s["tab_ok"], 2)
            dve.wait_ge(s["b2_ok"], 1)

            def pick(v, i, r, w):
                n = i * UNROLL + r
                return v[:, n * w:(n + 1) * w] if isinstance(n, int) else v[:, bass.ds(n * w, w)]

            def x_evac_tile(i, r):
                wait(dve, "xT_t", UNROLL, i, r + 1)
                wait(dve, "h_t", UNROLL, i, r - 1)
                dve.tensor_copy(xgT[:, r % 2, :], xT_bank[r % 2][:, 0:P]).then_inc(s["xT_e"], 1)

            def relu(i, r, x_e):
                wait(dve, "h_t", UNROLL, i, r + 1)
                wait(dve, "y_t", UNROLL, i, r - 1)
                cube = [P, HT, P]
                dve.tensor_tensor(hidT[:, r % 2, :].rearrange("p (j n) -> p j n", j=HT),
                                  h_bank[r % 2].rearrange("p (j n) -> p j n", j=HT),
                                  over(nb1[:, bass.ds(x_e * HT, HT)].unsqueeze(2), cube), ALU.max)\
                    .then_inc(s["h_e"], 1)

            def target_1(i, r):
                wait(dve, x_in_sem[r % RING_X], 16, i, 16)
                wait(dve, y_sem[r], 16, i, 0)
                dve.tensor_tensor(first_pick[:, r, :], xg[:, r, P:P + 1], pick(e_w, i, r, 1), ALU.is_equal)
                dve.scalar_tensor_tensor(out=spare[:, r, :], in0=xg[:, r, P:P + 1], scalar=0.0,
                                         in1=pick(spare_f, i, r, 1), op0=ALU.is_lt, op1=ALU.mult)\
                    .then_inc(s["pick1"], 1)

            def target_2(i, r):
                wait(dve, "pick1", UNROLL, i, r + 1)
                dve.scalar_tensor_tensor(out=first_pick[:, r, :], in0=first_pick[:, r, :], scalar=-float(ROWS),
                                         in1=xg[:, r, P + 1:XW], op0=ALU.mult, op1=ALU.add)\
                    .then_inc(s["pick2"], 1)

            def target_3(i, r):
                wait(dve, "pick2", UNROLL, i, r + 1)
                dve.tensor_tensor(y_at[:, r, :], first_pick[:, r, :], spare[:, r, :], ALU.add)\
                    .then_inc(s["y_at_ok"], 1)

            def output(i, r, x_e):
                wait(dve, "y_t", UNROLL, i, r + 1)
                dve.tensor_tensor(y_row[:, r, :], y_bank[r % 2][:, 0:P], b2_bc[:, bass.ds(x_e * P, P)], ALU.add)\
                    .then_inc(s["y_e"], 1)

            def steps(i, head, tail):
                x_e = entries(mybir.EngineType.DVE, tab_e, i, EXP - 1, 1 if tail else UNROLL + 1)
                for r in range(UNROLL):
                    if not tail:
                        target_1(i, r)
                        relu(i, r, x_e[r + 1])
                        target_2(i, r)
                    if not (head and r < 1) and not (tail and r > 0):
                        output(*back(i, r, 1), x_e[r])
                    if not tail:
                        target_3(i, r)
                        if not (r >= UNROLL - 2 and isinstance(i, int) and i == N_TILES // UNROLL - 1):
                            x_evac_tile(*((i, r + 2) if r < UNROLL - 2 else (i + 1, r + 2 - UNROLL)))

            x_evac_tile(0, 0)
            x_evac_tile(0, 1)
            tile_steps(dve, steps)

            def finish(b, r):
                wait(dve, y_in_sem[r], 32, b, 32)
                wait(dve, "fin_ok", 2, b, r - 1)

                def g(k, t):
                    return gate[:, 2 + k, bass.ds(b * 2 * LT + (r * LT + t), 1)]

                y_r = y_sum[:, r, :, :]
                for t in range(LT):
                    xt = x_all[:, bass.ds(b * 2 * LT + (r * LT + t), 1), :].rearrange("p a d -> p (a d)")
                    ins = dve.scalar_tensor_tensor(out=y_r[:, t, :], in0=y_back[:, r, 0, t, :], scalar=g(0, t),
                                                   in1=xt, op0=ALU.mult, op1=ALU.add)
                ins.then_inc(s["sum1"], 1)
                wait(dve, "sum1", 2, b, r + 1)
                for t in range(LT):
                    ins = dve.scalar_tensor_tensor(out=y_r[:, t, :], in0=y_back[:, r, 1, t, :], scalar=g(1, t),
                                                   in1=y_r[:, t, :], op0=ALU.mult, op1=ALU.add)
                ins.then_inc(s["sum2"], 1)
                wait(dve, "sum2", 2, b, r + 1)
                for t in range(LT):
                    ins = dve.bn_stats(stats_f[:, r, t, :], y_r[:, t, :])
                ins.then_inc(s["fin_stat"], 1)
                hold(dve, "fin_stat", 2, b, r + 1)
                for t in range(LT):
                    ins = dve.bn_aggr(mv_f[:, r, t, :], stats_f[:, r, t, :])
                ins.then_inc(s["fin_aggr"], 1)

            dve.wait_ge(s["x_kept"], BATCH)
            dve.wait_ge(s["gates_ok"], 1)
            for r in range(2):
                finish(0, r)
            with dve.Fori(1, BATCH // 2) as b:
                for r in range(2):
                    finish(b, r)

        @block.gpsimd
        def _(pool):
            pool.memset(v_pad[:, :, :, :], 0.0).then_inc(s["v_zero"], 1)
            pool.memset(kv_pad[:, :, :, :], 0.0).then_inc(s["v_zero"], 1)

            def split(b, side):
                wait(pool, "kq"[side] + "_ev", 1, b, 1)
                f = qk_f[:, side, :]
                p = parts[:, side, :, :]
                n = 3 * side
                pool.tensor_tensor(f, f, p[:, 0, :], ALU.subtract).then_inc(s["split"], 1)
                hold(pool, "split", 6, b, n + 1)
                pool.tensor_copy(p[:, 1, :], f).then_inc(s["split"], 1)
                wait(pool, "split", 6, b, n + 2)
                pool.tensor_tensor(p[:, 2, :], f, p[:, 1, :], ALU.subtract).then_inc(s["split"], 1)

            def square(b, u):
                if u % UNITS not in POOL_SQ:
                    return
                wait(pool, "sines", UNITS, b, u + 1)
                f = feats[:, u % HALF, 1, :]
                pool.tensor_tensor(f, f, f, ALU.mult).then_inc(s["sq_p"], 1)

            def rsqrt(per, n, base):
                wait(pool, "ln_aggr", per, n, base + 1)
                pool.tensor_tensor(rstd[:, :], mv[:, :, 1], eps_t[:, :], ALU.add).then_inc(s["ln_eps"], 1)
                wait(pool, "ln_eps", per, n, base + 1)
                pool.tensor_tensor(rstd[:, :], rstd[:, :], half_t[:, :], ALU.pow).then_inc(s["ln_pow"], 1)

            split(0, 0)
            split(0, 1)
            pool.wait_ge(s["wload"], 16 * N_WLOADS)

            def body(b, ph):
                first = isinstance(b, int) and b == 0
                last = isinstance(b, int) and b == BATCH - 1
                for u in range(UNITS):
                    if not (first and u < 2):
                        square(b, u - 2)
                    if first and u % 2 == 1:
                        t = u // 2 * LT
                        xb = x_all[:, t:t + LT, :]
                        pool.tensor_tensor(xb, xb, bo_bc[:, :, :], ALU.add).then_inc(s["bo_ok"], 1)
                    if u == 6 and not first:
                        rsqrt(1, b - 1, 0)
                    if u in (7, 9) and not last:
                        split(b + 1, (u - 7) // 2)
                    if u in (14, 15) and not first:
                        send_rows(b - 1, u - 14)

            def send_rows(b, k):
                hold(pool, "slots_ok", 1, b, 1)
                hold(pool, "meta", 1, b, 1)
                for t in range(LT):
                    pool.indirect_dma_start(routed_dram, bass.IndirectOffsetOnAxis(slots[:, k, t:t + 1], 0),
                                            rows_s[:, t, :], None).then_inc(s["scattered"], 16)

            sequences(pool, body)
            square(BATCH, -2)
            square(BATCH, -1)
            rsqrt(1, BATCH - 1, 0)
            for k in range(TOPK):
                send_rows(BATCH - 1, k)
            pool.wait_ge(s["rt"], 3)
            for e in range(EXP + 1):
                pool.indirect_dma_start(routed_dram, bass.IndirectOffsetOnAxis(pad_at[:, e:e + 1], 0),
                                        pad_rows[:, :], None).then_inc(s["pads_in"], 16)

            def steps(i, head, tail):
                for r in range(UNROLL):
                    if not (head and r < 1) and not (tail and r > 0):
                        j, q = back(i, r, 1)
                        hold(pool, "y_e", UNROLL, j, q + 1)
                        hold(pool, "y_at_ok", UNROLL, j, q + 1)
                        pool.indirect_dma_start(expert_dram, bass.IndirectOffsetOnAxis(y_at[:, q, :], 0),
                                                y_row[:, q, :], None).then_inc(y_sem[q], 16)

            tile_steps(pool, steps)

            def scale_and_shift(b, r):
                wait(pool, "fin_aggr", 2, b, r + 1)
                hold(pool, "fin_ok", 2, b, r - 1)
                pool.tensor_tensor(rstd_f[:, r, :], mv_f[:, r, :, 1], eps_t[:, :], ALU.add)\
                    .then_inc(s["fin_eps"], 1)
                wait(pool, "fin_eps", 2, b, r + 1)
                pool.tensor_tensor(rstd_f[:, r, :], rstd_f[:, r, :], half_t[:, :], ALU.pow)\
                    .then_inc(s["fin_rstd"], 1)
                wait(pool, "fin_rstd", 2, b, r + 1)
                pool.tensor_tensor(shift_f[:, r, :], mv_f[:, r, :, 0], rstd_f[:, r, :], ALU.mult)\
                    .then_inc(s["fin_mean"], 1)
                wait(pool, "fin_mean", 2, b, r + 1)
                pool.tensor_tensor(shift_f[:, r, :], zero_t[:, :], shift_f[:, r, :], ALU.subtract)\
                    .then_inc(s["fin_shift"], 1)

            for r in range(2):
                scale_and_shift(0, r)
            with pool.Fori(1, BATCH // 2) as b:
                for r in range(2):
                    scale_and_shift(b, r)


_INS = ["attn_x", "attn_proj_mat", "attn_Wq", "attn_bq", "attn_Wk", "attn_bk", "attn_Wv", "attn_bv", "attn_Wo",
        "attn_bo", "ffn_W1", "ffn_b1", "ffn_W2", "ffn_b2", "ffn_Wr", "ffn_br"]


def constants():
    import numpy as np
    mask = np.zeros((STK, SPL), np.float32)
    for r in range(STK):
        mask[r, r // (SPL * DH)] = 1.0
    tri = np.triu(np.ones((P, P), np.float16), 1)
    tok = np.zeros((P, LT, 2), np.float32)
    tok[:, :, 1] = ROWS - LEN + np.arange(LT) * P + np.arange(P)[:, None]
    pad = np.zeros((P, XW), np.float32)
    pad[:, P] = -1.0
    pad[:, P + 1] = TOPK * ROWS + np.arange(P)
    return [np.eye(P, dtype=np.float32), -np.eye(P, dtype=np.float16), mask,
            np.arange(EXP, dtype=np.float32), np.arange(EXP, dtype=np.float32) * REGION,
            np.arange(N_TILES, dtype=np.float32), tri, tok, pad]


def kernel(**inputs):
    import numpy as _np
    import concourse.bacc as _bacc
    from concourse import mybir as _mybir
    from concourse.bass_utils import run_bass_kernel_spmd as _run

    nc = _bacc.Bacc("TRN2", target_bir_lowering=False, num_devices=1)
    arrays, args = {}, []
    every = [(n, _np.ascontiguousarray(inputs["L0_" + n])) for n in _INS]
    every += [(f"const{i}", c) for i, c in enumerate(constants())]
    for name, a in every:
        arrays[name] = a
        args.append(nc.dram_tensor(name, a.shape, _mybir.dt.from_np(a.dtype), kind="ExternalInput").ap())
    args.append(nc.dram_tensor("out", (BATCH, LEN, P), F32, kind="ExternalOutput").ap())
    build(nc, *args)
    r = _run(nc, [arrays], core_ids=[0])
    return r.results[0]["out"]
```

```python
import math
from contextlib import ExitStack

import concourse.bass as bass
from concourse import mybir

F32 = mybir.dt.float32
U32 = mybir.dt.uint32
BF16 = mybir.dt.bfloat16
F16 = mybir.dt.float16
ALU = mybir.AluOpType
ACT = mybir.ActivationFunctionType
AX = mybir.AxisListType

P = 128
BATCH, LEN = 8, 512
LT = LEN // P
TILES = BATCH * LT
HEADS, DH = 16, 8
HG = 4
G = HEADS // HG
PADH = P // G
FEAT = 128
SPL = 3
PADW = PADH + DH
STK = SPL * SPL * DH
EXP, HID, HT = 8, 512, 4
UC = 1024
UNITS = 2 * HG * G * LEN // UC
HALF = UNITS // 2
RING = 3
KV_STEP = [4, 5, 6, 7, 8, 9, 10, 11]
N_LOADS = 6
N_WLOADS = 11
N_SETUP = 9
POOL_SQ = (1, 3, 4, 6, 8, 10, 12)
TURN = 1.0 / (2.0 * math.pi * math.sqrt(DH))
MAGIC = 12582912.0
TWO_PI = 6.2831850051879883
EPS = 1e-5
KV_SCALE = 1.0 / FEAT
MAGIC_LAST = 0.5 - 1.0 / 256
TOPK = 2
ROWS = BATCH * LEN
REGION = ROWS + P
XW = P + 2
N_TILES = 72
UNROLL = 8
Y_RING = 4
RING_X = UNROLL

AT_W2, AT_B2, AT_B1 = HID, 2 * HID, 2 * HID + P
WROW = AT_B1 + HT
EARLY = HG * G * LEN // 2 // WROW
W_RING = 4


def slot(phase, u):
    return (UNITS * phase + u) % RING


def before(u, pool):
    return sum((x in POOL_SQ) == pool for x in range(u))


def build(nc, x, proj, Wq, bq, Wk, bk, Wv, bv, Wo, bo, W1, b1, W2, b2, Wr, br,
          c_ident, c_negi, c_mask, c_iota, c_base, c_tile, c_tri, c_tok, c_pad, out):
    parts_dram = nc.dram_tensor("parts_dram", [BATCH, 2, SPL, P, LEN], BF16).ap()
    routed_dram = nc.dram_tensor("routed_dram", [(EXP + 1) * REGION, XW], F32).ap()
    expert_dram = nc.dram_tensor("expert_dram", [TOPK * ROWS + N_TILES * P, P], F32).ap()
    x_rows = x.rearrange("b (t p) d -> b p t d", p=P)
    out_rows = out.rearrange("b (t p) d -> b p t d", p=P)

    ctx = ExitStack()
    with ctx:
        def sb(name, shape, dt=F32):
            return ctx.enter_context(nc.sbuf_tensor(name, shape, dt))

        def sem(name):
            return ctx.enter_context(nc.semaphore(name))

        ident = sb("ident", [P, P])
        negi = sb("negi", [P, P], F16)
        mask = sb("mask", [STK, SPL])
        ident4 = sb("ident4", [P, P])
        minus_2 = sb("minus_2", [P, P])
        minus_half = sb("minus_half", [P, 2])
        w_raw = sb("w_raw", [P, 4, P])
        wo_perm = sb("wo_perm", [P, P])
        wT = sb("wT", [P, 3, P])
        woT = sb("woT", [P, P])
        bqk = sb("bqk", [2, P])
        bqk_p = sb("bqk_p", [2, P])
        bqk_t = sb("bqk_t", [P, 2])
        bv_raw = sb("bv_raw", [P, P])
        bv_bc = sb("bv_bc", [P, LT, P])
        bo_bc = sb("bo_bc", [P, LT, P])
        pr = sb("pr", [STK, 3, FEAT])
        prb = sb("prb", [STK, 3, FEAT], BF16)
        proj_stk = sb("proj_stk", [STK, FEAT], BF16)
        wr_s = sb("wr_s", [P, EXP])
        br_bc = sb("br_bc", [P, EXP])
        iota = sb("iota", [P, EXP])
        base = sb("base", [P, EXP])
        base_0 = sb("base_0", [P, EXP])
        tile_no = sb("tile_no", [P, N_TILES])
        tri = sb("tri", [P, P], F16)
        ones_b = sb("ones_b", [P, P], F16)
        pad_rows = sb("pad_rows", [P, XW])
        rows_s = sb("rows_s", [P, LT, XW])
        ends_u = sb("ends_u", [P, EXP], U32)
        xr_T = sb("xr_T", [P, LEN])
        lg = sb("lg", [P, LT, EXP])
        top8 = sb("top8", [P, LT, EXP])
        idx8 = sb("idx8", [P, LT, EXP], U32)
        hot = sb("hot", [P, TOPK, LT, EXP])
        picks = sb("picks", [P, LT * EXP], F16)
        slot_m = sb("slot_m", [P, LT, EXP])
        slot_k = sb("slot_k", [P, TOPK, LT, EXP])
        slots = sb("slots", [P, TOPK, LT], U32)
        best = sb("best", [P, TILES, TOPK])
        b1_raw = sb("b1_raw", [EXP * HT, P])
        b1_s = sb("b1_s", [P, EXP * HT])
        b2_s = sb("b2_s", [EXP, P])
        eps_t = sb("eps_t", [P, LT])
        half_t = sb("half_t", [P, LT])
        zero_t = sb("zero_t", [P, LT])
        warm = sb("warm", [P, LT])
        x_all = sb("x_all", [P, TILES, P])
        x_in = sb("x_in", [P, LT, P])
        xT = sb("xT", [P, LEN])
        qk_f = sb("qk_f", [P, 2, LEN])
        parts = sb("parts", [P, 2, SPL, LEN], BF16)
        weights_mem = sb("weights_mem", [P, EXP * WROW])
        stk = weights_mem[0:STK, 0:HG * G * LEN].bitcast(BF16).rearrange("p (s a g n) -> p s a g n", s=2, a=HG, g=G)
        v_pad = sb("v_pad", [P, LT, G, HG * PADW])
        turns = sb("turns", [P, 2, UC], F16)
        feats = sb("feats", [P, HALF, 2, UC])
        kvT = sb("kvT", [P, 2, FEAT])
        c_sum = sb("c_sum", [P, 1])
        kv_c = sb("kv_c", [P, P])
        kv_pad = sb("kv_pad", [P, 2, G, HG * PADW])
        outT = sb("outT", [P, LEN])
        y = sb("y", [P, LT, P])
        stats = sb("stats", [P, LT, 6])
        mv = sb("mv", [P, LT, 2])
        rstd = sb("rstd", [P, LT])
        fflat = feats[:, :, :, :].rearrange("p a b c -> p (a b c)")
        experts = weights_mem[:, :].rearrange("p (e n) -> p e n", e=EXP)
        free_at = [0]

        def take(n):
            free_at[0] += n
            return fflat[:, free_at[0] - n:free_at[0]]

        w_now = take(W_RING * WROW).rearrange("p (r n) -> p r n", r=W_RING)
        xg = take(RING_X * XW).rearrange("p (r n) -> p r n", r=RING_X)
        xgT = take(2 * P).rearrange("p (r n) -> p r n", r=2)
        hidT = take(2 * HID).rearrange("p (r n) -> p r n", r=2)
        y_row = take(UNROLL * P).rearrange("p (r n) -> p r n", r=UNROLL)
        first_pick = take(UNROLL).rearrange("p (r n) -> p r n", r=UNROLL)
        spare = take(UNROLL).rearrange("p (r n) -> p r n", r=UNROLL)
        y_at = take(UNROLL).rearrange("p (r n) -> p r n", r=UNROLL).bitcast(U32)
        ended = take(N_TILES * EXP).rearrange("p (i e) -> p i e", i=N_TILES)
        tiles_f = take(4 * EXP).rearrange("p (k e) -> p k e", k=4)
        tab_f = take(6 * N_TILES).rearrange("p (k i) -> p k i", k=6)
        tab_row = take(N_TILES).bitcast(U32)
        tab_e = take(N_TILES).bitcast(U32)
        gate = take(4 * TILES).rearrange("p (k t) -> p k t", k=4)
        y_back = take(Y_RING * TOPK * LEN).rearrange("p (r k t d) -> p r k t d", r=Y_RING, k=TOPK, t=LT)
        y_sum = take(2 * LEN).rearrange("p (r t d) -> p r t d", r=2, t=LT)
        stats_f = take(2 * LT * 6).rearrange("p (r t n) -> p r t n", r=2, t=LT)
        mv_f = take(2 * LT * 2).rearrange("p (r t n) -> p r t n", r=2, t=LT)
        rstd_f = take(2 * LT).rearrange("p (r t) -> p r t", r=2)
        shift_f = take(2 * LT).rearrange("p (r t) -> p r t", r=2)
        y_fin = take(2 * LEN).rearrange("p (r t d) -> p r t d", r=2, t=LT)

        ang = ctx.enter_context(nc.psum_tensor("ang", [P, 3, UC], F32))
        misc = ctx.enter_context(nc.psum_tensor("misc", [P, 2, 512], F32))

        banks = [ang[:, i // 2, (i % 2) * 512:(i % 2) * 512 + 512] for i in range(6)] + \
                [misc[:, i, :] for i in range(2)]
        xT_bank, h_bank, y_bank = banks[0:2], banks[2:4], banks[6:8]

        s = {n: sem(n) for n in (
            "loads", "loads_2", "wload", "xload", "xin_in", "v_zero", "consts",
            "raw_T", "raw_ev", "pad_ok", "setup",
            "angles", "rounded", "reduced", "sines", "sq_v", "sq_p",
            "xT_mm", "xT_ev", "q_mm", "q_ev", "k_mm", "k_ev", "v_mm", "v_ev", "split", "parts_out",
            "kvT_mm", "kvT_ev", "kv_mm", "kv_ev", "c_mm", "c_ev", "out_mm", "out_ev", "wo_mm",
            "y_ok", "bo_ok", "ln_stat", "ln_aggr", "ln_eps", "ln_pow", "xn_ok", "x_kept", "xr_mm", "xr_ev",
            "lg_mm", "lg_ok", "top_ok", "idx_ok", "hot_ok", "picked", "meta", "rk_mm", "slot_ok", "based",
            "slotk_ok", "slots_ok", "scattered", "pads_at", "pads_in", "rt", "tab_ok",
            "w1_in", "b1_mm", "b1_ok", "b2_mm", "b2_ok", "gap_ok", "gap_exp", "gates_ok",
            "xT_t", "xT_e", "h_t", "h_e", "y_t", "y_e", "w_ok", "pick1", "pick2", "y_at_ok",
            "first_ok", "sum1", "sum2", "fin_stat", "fin_aggr", "fin_eps", "fin_rstd", "fin_mean", "fin_shift",
            "fin_ok",
            "held",
        )}
        stk_in = [[sem(f"stk_in{side}{g}") for g in range(HG)] for side in range(2)]
        w2_in = [sem(f"w2_in{part}") for part in range(2)]
        x_in_sem = [sem(f"x_tile_in{r}") for r in range(RING_X)]
        y_sem = [sem(f"y_sent{r}") for r in range(UNROLL)]
        fin_sem = [sem(f"stored{r}") for r in range(2)]
        y_in_sem = [sem(f"y_in{r}") for r in range(Y_RING)]
        block = ctx.enter_context(nc.Block())

        def wait(eng, name, per, b, off):
            sm = s[name] if isinstance(name, str) else name
            if isinstance(b, int):
                if per * b + off > 0:
                    eng.wait_ge(sm, per * b + off)
            else:
                eng.wait_ge(sm, b * per + off)

        def hold(eng, name, per, b, off):
            wait(eng, name, per, b, off)
            if not isinstance(b, int):
                eng.sem_inc(s["held"], 1)

        def back(i, r, n):
            return (i, r - n) if r >= n else (i - 1, r - n + UNROLL)

        def dense(pads):
            return pads.rearrange("p n (a w) -> p n a w", a=HG)[:, :, :, 0:DH]

        def gate_of(k, n, t):
            return gate[:, 2 + k, n * LT + t:n * LT + t + 1]

        def tile_steps(eng, steps):
            last = N_TILES // UNROLL
            steps(0, True, False)
            with eng.Fori(1, last - 1) as i:
                steps(i, False, False)
            steps(last - 1, False, False)
            steps(last, False, True)

        def entries(engine, table, i, most):
            cols = table[0:1, i * UNROLL:(i + 1) * UNROLL] if isinstance(i, int) \
                else table[0:1, bass.ds(i * UNROLL, UNROLL)]
            return nc.values_load_multi_w_load_instructions(cols, engines=[engine], min_val=0, max_val=most)[1]

        def sequences(eng, body):
            body(0, 0)
            with eng.Fori(0, (BATCH - 2) // RING) as i:
                for r in range(RING):
                    body(i * RING + (r + 1), (r + 1) % RING)
            body(BATCH - 1, (BATCH - 1) % RING)

        def split(eng, b, side):
            wait(eng, "kq"[side] + "_ev", 1, b, 1)
            f = qk_f[:, side, :]
            p = parts[:, side, :, :]
            n = 3 * side
            eng.tensor_tensor(f, f, p[:, 0, :], ALU.subtract).then_inc(s["split"], 1)
            hold(eng, "split", 6, b, n + 1)
            eng.tensor_copy(p[:, 1, :], f).then_inc(s["split"], 1)
            wait(eng, "split", 6, b, n + 2)
            eng.tensor_tensor(p[:, 2, :], f, p[:, 1, :], ALU.subtract).then_inc(s["split"], 1)

        @block.sync
        def _(sp):
            for dst, src in ((ident[:, :], c_ident), (w_raw[:, 0, :], Wk), (w_raw[:, 1, :], Wq),
                             (w_raw[:, 2, :], Wv), (bqk[0:1, :], bk.unsqueeze(0)), (bqk[1:2, :], bq.unsqueeze(0))):
                sp.dma_start(dst, src).then_inc(s["loads"], 16)
            sp.dma_start(x_in[:, :, :], x_rows[0]).then_inc(s["xin_in"], 16)
            for dst, src in (
                (mask[:, :], c_mask), (pr[:, 0, :], proj.unsqueeze(0).broadcast_to([SPL * SPL, DH, FEAT])),
                (bv_raw[:, :], bv.partition_broadcast(P)), (negi[:, :], c_negi), (w_raw[:, 3, :], Wo),
                (bo_bc[:, :, :], bo.unsqueeze(0).unsqueeze(0).broadcast_to([P, LT, P])),
            ):
                sp.dma_start(dst, src).then_inc(s["loads_2"], 16)

            def stack(b):
                def write(side):
                    hold(sp, "split", 6, b, 3 * side + 3)
                    dst = parts_dram[b, side].rearrange("i r n -> r i n")
                    sp.dma_start(dst, parts[:, side, :, :]).then_inc(s["parts_out"], 16)
                    hold(sp, "parts_out", 32, b, 16 * side + 16)

                def read(side, hg):
                    hold(sp, "angles", UNITS, b, HALF * side + 2 * hg + 2 - UNITS)
                    rows = parts_dram[b, side].rearrange("i (d h) n -> (i d) (h n)", d=DH)
                    src = rows[:, hg * G * LEN:(hg + 1) * G * LEN]
                    sp.dma_start(stk[:, side, hg, :, :].rearrange("p g n -> p (g n)"),
                                 src.unsqueeze(0).broadcast_to([SPL, SPL * DH, G * LEN]))\
                        .then_inc(stk_in[side][hg], 16)

                for side in range(2):
                    write(side)
                    for hg in range(HG):
                        read(side, hg)

            def load_x(b):
                hold(sp, "xT_mm", 1, b, 0)
                sp.dma_start(x_in[:, :, :], x_rows[b]).then_inc(s["xin_in"], 16)

            load_x(1)
            stack(0)
            for t in range(BATCH):
                sp.dma_start(x_all[:, t * LT:(t + 1) * LT, :], x_rows[t]).then_inc(s["xload"], 16)
            sp.dma_start(wr_s[:, :], Wr).then_inc(s["wload"], 16)
            sp.dma_start(br_bc[:, :], br.partition_broadcast(P)).then_inc(s["wload"], 16)
            for dst, src in ((iota[:, :], c_iota.partition_broadcast(P)), (base[:, :], c_base.partition_broadcast(P)),
                             (base_0[:, :], c_base.partition_broadcast(P)), (tile_no[:, :], c_tile.partition_broadcast(P)),
                             (tri[:, :], c_tri), (pad_rows[:, :], c_pad)):
                sp.dma_start(dst, src).then_inc(s["wload"], 16)
            sp.dma_start(rows_s[:, :, P:XW], c_tok).then_inc(s["wload"], 16)
            sp.dma_start(b1_raw[:, :], b1.rearrange("e (j p) -> (e j) p", p=P)).then_inc(s["wload"], 16)
            sp.dma_start(b2_s[:, :], b2).then_inc(s["wload"], 16)
            with sp.Fori(1, BATCH - 1) as b:
                load_x(b + 1)
                stack(b)
            stack(BATCH - 1)
            sp.dma_start(routed_dram[EXP * REGION:EXP * REGION + P, :], pad_rows[:, :]).then_inc(s["pads_in"], 16)
            for part, (lo, hi) in enumerate(((0, EARLY), (EARLY, EXP))):
                sp.wait_ge(s["angles"], UNITS * (BATCH - 1) + HALF * (part + 1))
                for x_e in range(lo, hi):
                    sp.dma_start(experts[:, x_e, AT_W2:AT_B2].rearrange("p (j d) -> p j d", j=HT),
                                 W2[x_e].rearrange("(j p) d -> p j d", p=P)).then_inc(w2_in[part], 16)
                sp.dma_start(experts[:, lo:hi, 0:HID], W1[lo:hi].rearrange("e d h -> d e h")).then_inc(s["w1_in"], 16)
            sp.wait_ge(s["pads_at"], 1)
            ends = nc.values_load_multi_w_load_instructions(
                ends_u[0:1, :], engines=[mybir.EngineType.SP], min_val=0, max_val=EXP * REGION - P)[1]
            for end in ends:
                sp.dma_start(routed_dram[bass.ds(end, P), :], pad_rows[:, :]).then_inc(s["pads_in"], 16)
            sp.wait_ge(s["tab_ok"], 2)
            rows = entries(mybir.EngineType.SP, tab_row, 0, (EXP + 1) * REGION - P)
            sp.wait_ge(s["scattered"], 16 * TOPK * TILES)
            sp.wait_ge(s["pads_in"], 16 * (EXP + 1))

            def load_tile(i, r, row):
                if not isinstance(i, int):
                    hold(sp, "xT_t", UNROLL, i, r + 1 - RING_X)
                    hold(sp, "y_at_ok", UNROLL, i, r + 1 - RING_X)
                sp.dma_start(xg[:, r, :], routed_dram[bass.ds(row, P), :]).then_inc(x_in_sem[r], 16)

            for r in range(UNROLL):
                load_tile(0, r, rows[r])
            with sp.Fori(1, N_TILES // UNROLL) as i:
                rows = entries(mybir.EngineType.SP, tab_row, i, (EXP + 1) * REGION - P)
                for r in range(UNROLL):
                    load_tile(i, r, rows[r])
            for r in range(UNROLL):
                sp.wait_ge(y_sem[r], 16 * N_TILES // UNROLL)
            back = expert_dram[0:TOPK * ROWS, :].rearrange("(k b t p) d -> b k p t d", k=TOPK, t=LT, p=P)

            for n in range(BATCH + Y_RING):
                if n < BATCH:
                    if n >= Y_RING:
                        sp.wait_ge(s["sum2"], n - Y_RING + 1)
                    for k in range(TOPK):
                        sp.dma_start(y_back[:, n % Y_RING, k, :, :], back[n, k]).then_inc(y_in_sem[n % Y_RING], 16)
                if n >= Y_RING:
                    m = n - Y_RING
                    sp.wait_ge(s["fin_ok"], m + 1)
                    sp.dma_start(out_rows[m], y_fin[:, m % 2, :, :]).then_inc(fin_sem[m % 2], 16)
            for r in range(2):
                sp.wait_ge(fin_sem[r], 16 * BATCH // 2)

        @block.tensor
        def _(pe):
            pe.wait_ge(s["loads"], 16 * N_LOADS)
            for i in range(3):
                mm = pe.transpose(misc[:, 0, i * P:(i + 1) * P], w_raw[:, i, :], ident[:, :])
            pe.wait_ge(s["pad_ok"], 1)
            mm = pe.transpose(misc[:, 0, 3 * P:3 * P + 2], bqk_p[:, :], ident[0:2, 0:2])
            mm.then_inc(s["raw_T"], 1)
            def x_T(b, *free):
                wait(pe, "xin_in", 16, b, 16)
                wait(pe, *free)
                for t in range(LT):
                    mm = pe.transpose(misc[:, 0, t * P:(t + 1) * P], x_in[:, t, :], ident[:, :])
                mm.then_inc(s["xT_mm"], 1)

            def project(side, bank, b, *free):
                wait(pe, "xT_ev", 1, b, 1)
                wait(pe, *free)
                pe.matmul(misc[:, bank, :], wT[:, side, :], xT[:, :], start=True, stop=True)\
                    .then_inc(s["kq"[side] + "_mm"], 1)

            def v_product(b, bank, *free):
                wait(pe, *free)
                for t in range(LT):
                    mm = pe.matmul(misc[:, bank, t * P:(t + 1) * P], xT[:, t * P:(t + 1) * P], wT[:, 2, :],
                                   start=True, stop=True)
                mm.then_inc(s["v_mm"], 1)

            x_T(0, "raw_ev", 0, 0, 1)
            project(0, 1, 0, "raw_ev", 0, 0, 1)
            project(1, 0, 0, "xT_ev", 0, 0, 1)
            v_product(0, 1, "k_ev", 0, 0, 1)
            pe.wait_ge(s["pad_ok"], 2)
            pe.wait_ge(s["q_ev"], 1)
            pe.transpose(misc[:, 0, 0:P], wo_perm[:, :], ident[:, :]).then_inc(s["raw_T"], 1)

            def angles(b, ph, u):
                side, hg, half = u // HALF, u % HALF // 2, u % 2
                if half == 0:
                    wait(pe, stk_in[side][hg], 16, b, 16)
                wait(pe, "sines", UNITS, b, u - RING + 1)
                a = ang[:, slot(ph, u), :]
                if side == 0:
                    for t in range(2):
                        for g in range(G):
                            at = (t * G + g) * FEAT
                            tok = (2 * half + t) * P
                            mm = pe.matmul(a[:, at:at + FEAT], stk[:, 0, hg, g, tok:tok + P], proj_stk[:, :],
                                           start=(g == 0), stop=False, skip_group_check=True)
                else:
                    for t in range(2):
                        mm = pe.matmul(a[:, t * 512:(t + 1) * 512], proj_stk[:, :],
                                       stk[:, 1, hg, 2 * half + t, :], start=True, stop=False,
                                       skip_group_check=True)
                mm.then_inc(s["angles"], 1)

            def reduce_turns(b, ph, u):
                wait(pe, "rounded", UNITS, b, u + 1)
                for t in range(2):
                    mm = pe.matmul(ang[:, slot(ph, u), t * 512:(t + 1) * 512], negi[:, :],
                                   turns[:, u % 2, t * 512:(t + 1) * 512], start=False, stop=True,
                                   skip_group_check=True)
                mm.then_inc(s["reduced"], 1)

            def squared(b, u):
                wait(pe, "sq_v", UNITS - len(POOL_SQ), b, before(u + 1, False))
                wait(pe, "sq_p", len(POOL_SQ), b, before(u + 1, True))

            def kv_product(b, u, *free):
                hg, half = u // 2, u % 2
                squared(b, u)
                if u == 0:
                    wait(pe, "v_ev", 1, b, 1)
                    wait(pe, *free)
                for t in range(2):
                    for g in range(G):
                        at = (t * G + g) * FEAT
                        mm = pe.matmul(misc[32 * g:32 * g + 32, 0, 0:2 * FEAT].rearrange("p (a m) -> p a m", a=2),
                                       v_pad[:, 2 * half + t, g, hg * PADH:(hg + 1) * PADH],
                                       feats[:, u, :, at:at + FEAT],
                                       start=(u == 0 and t == 0), stop=(u == HALF - 1 and t == 1),
                                       skip_group_check=True)
                mm.then_inc(s["kvT_mm"], 1)

            def kv_turn(b):
                wait(pe, "kvT_ev", 1, b, 1)
                o = misc[:, 0, :]
                pe.matmul(o[:, 0:P], kvT[:, 0, :], ident[:, :], start=True, stop=True, skip_group_check=True)
                pe.matmul(o[:, P:2 * P], kvT[:, 1, :], ident4[:, :], start=True, stop=False, skip_group_check=True)
                for t in range(LT):
                    mm = pe.matmul(o[:, P:2 * P], minus_2[:, :], dense(v_pad[:, t, :, :]),
                                   start=False, stop=(t == LT - 1), skip_group_check=True)
                mm.then_inc(s["kv_mm"], 1)

            def c_product(b):
                wait(pe, "kv_ev", 1, b, 1)
                pe.matmul(misc[:, 0, 2 * P:2 * P + 2], kv_c[:, :], minus_half[:, :], start=True, stop=True)\
                    .then_inc(s["c_mm"], 1)

            def out_product(b, hg, a, *free):
                u = HALF + 2 * hg
                if a == 0:
                    wait(pe, "sines", UNITS, b, u + 2)
                else:
                    squared(b, u + 1)
                if hg == 0 and a == 0:
                    wait(pe, "kv_ev", 1, b, 1)
                    wait(pe, *free)
                for g in range(G):
                    mm = pe.matmul(misc[32 * g:32 * g + 32, 1, :], kv_pad[:, a, g, hg * PADH:(hg + 1) * PADH],
                                   feats[:, 2 * hg + g // 2, a, (g % 2) * LEN:(g % 2 + 1) * LEN],
                                   start=(hg == 0 and a == 0), stop=(hg == HG - 1 and a == 1),
                                   skip_group_check=True)
                if a == 1:
                    mm.then_inc(s["out_mm"], 1)

            def wo_product(b):
                wait(pe, "out_ev", 1, b, 1)
                for t in range(LT):
                    mm = pe.matmul(misc[:, 1, t * P:(t + 1) * P], outT[:, t * P:(t + 1) * P], woT[:, :],
                                   start=True, stop=True)
                mm.then_inc(s["wo_mm"], 1)

            def rows_T(b, *free):
                wait(pe, "xn_ok", 1, b, 1)
                wait(pe, *free)
                for t in range(LT):
                    mm = pe.transpose(misc[:, 1, t * P:(t + 1) * P], rows_s[:, t, 0:P], ident[:, :])
                mm.then_inc(s["xr_mm"], 1)

            def logits(b, *free):
                wait(pe, "xr_ev", 1, b, 1)
                wait(pe, *free)
                for t in range(LT):
                    mm = pe.matmul(misc[:, 1, t * EXP:(t + 1) * EXP], xr_T[:, t * P:(t + 1) * P], wr_s[:, :],
                                   start=True, stop=True)
                mm.then_inc(s["lg_mm"], 1)

            def ranks(b, *free):
                wait(pe, "picked", 1, b, 1)
                wait(pe, *free)
                o = misc[:, 1, :]
                n = LT * EXP
                pe.matmul(o[:, 0:n], tri[:, :], picks[:, :], start=True, stop=False, skip_group_check=True)
                for t in range(1, LT):
                    pe.matmul(o[:, t * EXP:n], ones_b[:, :], picks[:, 0:n - t * EXP],
                              start=False, stop=False, skip_group_check=True)
                for t in range(LT):
                    mm = pe.matmul(o[:, n:n + EXP], ones_b[:, :], picks[:, t * EXP:(t + 1) * EXP],
                                   start=False, stop=(t == LT - 1), skip_group_check=True)
                mm.then_inc(s["rk_mm"], 1)

            def body(b, ph):
                first = isinstance(b, int) and b == 0
                last = isinstance(b, int) and b == BATCH - 1
                for u in range(UNITS):
                    angles(b, ph, u)
                    if not (first and u == 0):
                        reduce_turns(b, ph, u - 1)
                    if u == 0 and not first:
                        out_product(b - 1, 2, 0)
                    if u == 1 and not last:
                        x_T(b + 1, *(("raw_ev", 1, b, 2) if first else ("v_ev", 1, b, 1)))
                    if u == 1 and not first:
                        out_product(b - 1, 2, 1)
                    if u == 2 and not first:
                        out_product(b - 1, 3, 0)
                    if u == 3 and not first:
                        out_product(b - 1, 3, 1)
                    if u in KV_STEP:
                        kv_product(b, KV_STEP.index(u), *(("v_ev", 1, b, 1) if last else ("xT_ev", 1, b, 2)))
                    if u == 4 and not first:
                        wo_product(b - 1)
                    if u == 6 and not last:
                        project(0, 1, b + 1, *(("v_ev", 1, b, 1) if first else ("y_ok", 1, b, 0)))
                    if u == 7 and not last:
                        project(1, 1, b + 1, "k_ev", 1, b, 2)
                    if u == 8 and not first:
                        rows_T(b - 1, *(("y_ok", 1, b, 0) if last else ("q_ev", 1, b, 2)))
                    if u == 9 and not first:
                        logits(b - 1, "xr_ev", 1, b, 0)
                    if u == 12:
                        kv_turn(b)
                        if not first:
                            ranks(b - 1, "lg_ok", 1, b, 0)
                    if u == 13:
                        out_product(b, 0, 0, *(("q_ev", 1, b, 2) if first else ("based", 1, b, 0)))
                        out_product(b, 0, 1)
                    if u == 14:
                        c_product(b)
                        out_product(b, 1, 0)
                    if u == 15:
                        out_product(b, 1, 1)
                        if not last:
                            v_product(b + 1, 0, "c_ev", 1, b, 1)

            pe.wait_ge(s["setup"], N_SETUP)
            sequences(pe, body)
            e = BATCH
            reduce_turns(e, e % RING, -1)
            for hg in (2, 3):
                for a in range(2):
                    out_product(e - 1, hg, a)
            wo_product(e - 1)

            def expert_biases(lo, hi):
                if lo == 0:
                    pe.wait_ge(s["sines"], UNITS * BATCH)
                    pe.transpose(banks[5][:, 0:EXP * HT], b1_raw[:, :], ident[0:EXP * HT, 0:EXP * HT])\
                        .then_inc(s["b1_mm"], 1)
                    pe.wait_ge(s["b1_ok"], 1)
                for x_e in range(lo, hi):
                    if x_e in (0, EARLY):
                        part = (0, EARLY).index(x_e)
                        pe.wait_ge(w2_in[part], 16 * (EARLY, EXP - EARLY)[part])
                    o = banks[3 + x_e // 4][:, (x_e % 4) * P:(x_e % 4 + 1) * P]
                    pe.matmul(o, ident[0:EXP, x_e:x_e + 1].broadcast_to([EXP, P]), b2_s[:, :],
                              start=True, stop=False)
                    for j in range(HT):
                        mm = pe.matmul(o, b1_s[:, x_e * HT + j:x_e * HT + j + 1].broadcast_to([P, P]),
                                       experts[:, x_e, AT_W2 + j * P:AT_W2 + (j + 1) * P],
                                       start=False, stop=(j == HT - 1))
                mm.then_inc(s["b2_mm"], 1)

            expert_biases(0, EXP // 2)
            rows_T(e - 1, "y_ok", 1, e, 0)
            logits(e - 1, "xr_ev", 1, e, 0)
            ranks(e - 1, "lg_ok", 1, e, 0)

            expert_biases(EXP // 2, EXP)
            pe.wait_ge(s["based"], BATCH)

            def x_turn(i, r):
                wait(pe, x_in_sem[r % RING_X], 16, i, 16 * (r // RING_X) + 16)
                wait(pe, "xT_e", UNROLL, i, r - 1)
                pe.transpose(xT_bank[r % 2][:, 0:P], xg[:, r % RING_X, 0:P], ident[:, :]).then_inc(s["xT_t"], 1)

            def first_layer(i, r):
                wait(pe, "xT_e", UNROLL, i, r + 1)
                wait(pe, "w_ok", UNROLL, i, r + 1)
                wait(pe, "h_e", UNROLL, i, r - 1)
                for j in range(HT):
                    mm = pe.matmul(h_bank[r % 2][:, j * P:(j + 1) * P], w_now[:, r % W_RING, j * P:(j + 1) * P],
                                   xgT[:, r % 2, :], start=True, stop=True)
                mm.then_inc(s["h_t"], 1)

            def second_layer(i, r):
                wait(pe, "h_e", UNROLL, i, r + 1)
                wait(pe, "y_e", UNROLL, i, r - 1)
                for j in range(HT):
                    mm = pe.matmul(y_bank[r % 2][:, 0:P], hidT[:, r % 2, j * P:(j + 1) * P],
                                   w_now[:, r % W_RING, AT_W2 + j * P:AT_W2 + (j + 1) * P],
                                   start=(j == 0), stop=(j == HT - 1))
                mm.then_inc(s["y_t"], 1)

            def steps(i, head, tail):
                for r in range(UNROLL):
                    if not tail:
                        first_layer(i, r)
                    if not (head and r < 1) and not (tail and r > 0):
                        second_layer(*back(i, r, 1))
                    if not tail and not (r >= UNROLL - 2 and isinstance(i, int)
                                         and i == N_TILES // UNROLL - 1):
                        x_turn(i, r + 2)

            x_turn(0, 0)
            x_turn(0, 1)
            tile_steps(pe, steps)

        @block.scalar
        def _(act):
            def out_evac(b):
                wait(act, "out_mm", HG, b, HG)
                wait(act, "c_ev", 1, b, 1)
                wait(act, "wo_mm", 1, b, 0)
                act.activation(outT[:, :], misc[:, 1, :], ACT.Identity, bias=c_sum[:, :]).then_inc(s["out_ev"], 1)

            def proj_evac(b, side, bank):
                wait(act, "kq"[side] + "_mm", 1, b, 1)
                wait(act, "split", 6, b, 3 * side - 3)
                wait(act, "parts_out", 32, b, 16 * side - 16)
                act.activation(parts[:, side, 0, :], misc[:, bank, :], ACT.Identity,
                               bias=bqk_t[:, side:side + 1], scale=TURN)
                act.activation(qk_f[:, side, :], misc[:, bank, :], ACT.Identity,
                               bias=bqk_t[:, side:side + 1], scale=TURN).then_inc(s["kq"[side] + "_ev"], 1)

            def sines(b, ph, u):
                wait(act, "reduced", UNITS, b, u + 1)
                if u < HALF:
                    wait(act, "out_mm", HG, b, u // 2 + 1 - HG)
                else:
                    wait(act, "kvT_mm", HALF, b, u - HALF + 1)
                a = ang[:, slot(ph, u), :]
                f = feats[:, u % HALF, :, :]
                act.activation(f[:, 0, :], a, ACT.Sin, scale=TWO_PI)
                act.activation(f[:, 1, :], a, ACT.Sin, scale=TWO_PI / 2).then_inc(s["sines"], 1)

            def rows_evac(b):
                wait(act, "xr_mm", 1, b, 1)
                act.activation(xr_T[:, :], misc[:, 1, :], ACT.Copy).then_inc(s["xr_ev"], 1)

            def keep_rows(b):
                wait(act, "xn_ok", 1, b, 1)
                xb = x_all[:, b * LT:(b + 1) * LT, :] if isinstance(b, int) else x_all[:, bass.ds(b * LT, LT), :]
                act.activation(xb, rows_s[:, :, 0:P], ACT.Copy).then_inc(s["x_kept"], 1)

            act.wait_ge(s["consts"], 1)
            act.activation(warm[:, :], zero_t[:, :], ACT.Sin)
            act.wait_ge(s["setup"], 1)
            proj_evac(0, 0, 1)
            proj_evac(0, 1, 0)

            def body(b, ph):
                first = isinstance(b, int) and b == 0
                last = isinstance(b, int) and b == BATCH - 1
                for u in range(UNITS):
                    if u == 3 and not first:
                        out_evac(b - 1)
                    if u in (6, 7) and not last:
                        proj_evac(b + 1, u - 6, 1)
                    if u == 8 and not first:
                        rows_evac(b - 1)
                    if u == 10 and not first:
                        keep_rows(b - 1)
                    sines(b, ph, u)

            sequences(act, body)
            out_evac(BATCH - 1)

            act.wait_ge(s["b1_mm"], 1)
            b1_T = banks[5][:, 0:EXP * HT]
            act.activation(experts[:, :, AT_B1:WROW], b1_T.rearrange("p (e j) -> p e j", e=EXP), ACT.Copy,
                           scale=-1.0)
            act.activation(b1_s[:, :], b1_T, ACT.Copy).then_inc(s["b1_ok"], 1)

            rows_evac(BATCH - 1)
            keep_rows(BATCH - 1)
            for h in range(2):
                act.wait_ge(s["b2_mm"], h + 1)
                act.activation(experts[:, h * EXP // 2:(h + 1) * EXP // 2, AT_B2:AT_B1],
                               banks[3 + h].rearrange("p (e d) -> p e d", e=EXP // 2), ACT.Copy)\
                    .then_inc(s["b2_ok"], 1)
            act.wait_ge(s["gap_ok"], 1)
            act.activation(gate[:, 1, :], gate[:, 0, :], ACT.Exp).then_inc(s["gap_exp"], 1)
            act.wait_ge(s["w1_in"], 32)
            act.wait_ge(s["b2_ok"], 2)
            act.wait_ge(s["tab_ok"], 2)

            def weights(i, r, x_e):
                wait(act, "y_e", UNROLL, i, r + 1 - W_RING)
                act.activation(w_now[:, r % W_RING, :],
                               experts[:, bass.ds(x_e, 1), :].rearrange("p a n -> p (a n)"), ACT.Copy)\
                    .then_inc(s["w_ok"], 1)

            def steps(i, head, tail):
                if not tail:
                    x_e = entries(mybir.EngineType.Activation, tab_e, i, EXP - 1)
                    for r in range(UNROLL):
                        weights(i, r, x_e[r])

            tile_steps(act, steps)

            def first_scaled(n):
                act.wait_ge(y_in_sem[n % Y_RING], 32 * (n // Y_RING) + 32)
                for t in range(LT):
                    y_t = y_back[:, n % Y_RING, 0, t, :]
                    ins = act.activation(y_t, y_t, ACT.Copy, scale=gate_of(0, n, t))
                ins.then_inc(s["first_ok"], 1)

            def final_norm(n):
                act.wait_ge(s["fin_shift"], n + 1)
                if n >= 2:
                    act.wait_ge(fin_sem[n % 2], 16 * (n // 2))
                r = n % 2
                for t in range(LT):
                    ins = act.activation(y_fin[:, r, t, :], y_sum[:, r, t, :], ACT.Identity,
                                         bias=shift_f[:, r, t:t + 1], scale=rstd_f[:, r, t:t + 1])
                ins.then_inc(s["fin_ok"], 1)

            act.wait_ge(s["gates_ok"], 1)
            first_scaled(0)
            first_scaled(1)
            for n in range(BATCH):
                if n + 2 < BATCH:
                    first_scaled(n + 2)
                final_norm(n)

        @block.vector
        def _(dve):
            dve.memset(zero_t[:, :], 0.0).then_inc(s["consts"], 1)
            dve.memset(minus_2[:, :], -2.0)
            dve.memset(minus_half[:, :], -0.5)
            dve.memset(eps_t[:, :], EPS)
            dve.memset(ones_b[:, :], 1.0)
            dve.memset(half_t[:, :], -0.5)
            dve.wait_ge(s["loads"], 16 * N_LOADS)
            dve.tensor_copy(bqk_p[:, :].rearrange("p (d h) -> p d h", d=DH),
                            bqk[:, :].rearrange("p (h d) -> p d h", d=DH)).then_inc(s["pad_ok"], 1)
            dve.wait_ge(s["raw_T"], 1)
            for a in range(2):
                dve.tensor_copy(wT[:, a, :].rearrange("p (d h) -> p d h", d=DH),
                                misc[:, 0, a * P:(a + 1) * P].rearrange("p (h d) -> p d h", d=DH))
            dve.tensor_copy(wT[:, 2, :].rearrange("p (g a d) -> p g a d", a=HG, g=G),
                            misc[:, 0, 2 * P:3 * P].rearrange("p (a g d) -> p g a d", a=HG, g=G))
            dve.tensor_scalar(bqk_t[:, :], misc[:, 0, 3 * P:3 * P + 2], TURN, None, ALU.mult)\
                .then_inc(s["raw_ev"], 1)
            dve.wait_ge(s["raw_ev"], 1)
            dve.sem_inc(s["setup"], 1)

            def x_evac(b):
                wait(dve, "xT_mm", 1, b, 1)
                dve.tensor_copy(xT[:, :], misc[:, 0, :]).then_inc(s["xT_ev"], 1)

            x_evac(0)
            n_set = [1]

            def chain(ins):
                n_set[0] += 1
                ins.then_inc(s["setup"], 1)
                dve.wait_ge(s["setup"], n_set[0])

            dve.wait_ge(s["loads_2"], 16 * N_LOADS)
            for i in range(SPL):
                chain(dve.tensor_copy(prb[:, i, :], pr[:, i, :]))
                if i < SPL - 1:
                    chain(dve.tensor_tensor(pr[:, i + 1, :], pr[:, i, :], prb[:, i, :], ALU.subtract))
            chain(dve.tensor_scalar(pr[:, 0, :], prb[:, 0, :], mask[:, 0:1], None, ALU.mult))
            chain(dve.scalar_tensor_tensor(out=pr[:, 1, :], in0=prb[:, 1, :], scalar=mask[:, 1:2],
                                           in1=pr[:, 0, :], op0=ALU.mult, op1=ALU.add))
            chain(dve.scalar_tensor_tensor(out=proj_stk[:, :], in0=prb[:, 2, :], scalar=mask[:, 2:3],
                                           in1=pr[:, 1, :], op0=ALU.mult, op1=ALU.add))
            assert n_set[0] == N_SETUP
            for side in range(2):
                split(dve, 0, side)
            dve.tensor_scalar(ident4[:, :], ident[:, :], 4.0, None, ALU.mult)
            dve.tensor_copy(wo_perm[:, :].rearrange("p (g a d) -> p g a d", a=HG, g=G),
                            w_raw[:, 3, :].rearrange("p (a g d) -> p g a d", a=HG, g=G)).then_inc(s["pad_ok"], 1)
            for t in range(LT):
                dve.tensor_scalar(bv_bc[:, t, :].rearrange("p (g a d) -> p g a d", a=HG, g=G),
                                  bv_raw[:, :].rearrange("p (a g d) -> p g a d", a=HG, g=G), KV_SCALE, None,
                                  ALU.mult).then_inc(s["consts"], 1)

            def round_turns(b, ph, u):
                wait(dve, "angles", UNITS, b, u + 1)
                wait(dve, "reduced", UNITS, b, u - 1)
                dve.tensor_scalar(turns[:, u % 2, :], ang[:, slot(ph, u), :], MAGIC, -MAGIC, ALU.add, ALU.add)\
                    .then_inc(s["rounded"], 1)

            def square(b, u):
                if u % UNITS in POOL_SQ:
                    return
                wait(dve, "sines", UNITS, b, u + 1)
                f = feats[:, u % HALF, 1, :]
                dve.tensor_tensor(f, f, f, ALU.mult).then_inc(s["sq_v"], 1)

            def kvT_evac(b):
                wait(dve, "kvT_mm", HALF, b, HALF)
                dve.tensor_copy(kvT[:, :, :].rearrange("p a m -> p (a m)"), misc[:, 0, 0:2 * P])\
                    .then_inc(s["kvT_ev"], 1)

            def kv_evac(b):
                wait(dve, "kv_mm", 1, b, 1)
                wait(dve, "out_mm", HG, b, 0)
                dve.tensor_copy(kv_c[:, :], misc[:, 0, P:2 * P])
                dve.tensor_copy(dense(kv_pad[:, :, :, :].rearrange("p a g w -> p (a g) w")),
                                misc[:, 0, 0:2 * P].rearrange("p (g a d) -> p g a d", a=HG, d=DH))\
                    .then_inc(s["kv_ev"], 1)

            def c_evac(b):
                wait(dve, "c_mm", 1, b, 1)
                wait(dve, "out_ev", 1, b, 0)
                dve.tensor_copy(c_sum[:, :], misc[:, 0, 2 * P:2 * P + 1]).then_inc(s["c_ev"], 1)

            def v_evac(b, bank):
                wait(dve, "v_mm", 1, b, 1)
                dve.scalar_tensor_tensor(out=dense(v_pad[:, :, :, :].rearrange("p t g w -> p (t g) w")),
                                         in0=misc[:, bank, :].rearrange("p (g a d) -> p g a d", a=HG, d=DH),
                                         scalar=KV_SCALE,
                                         in1=bv_bc[:, :, :].rearrange("p t (g a d) -> p (t g) a d", a=HG, d=DH),
                                         op0=ALU.mult, op1=ALU.add).then_inc(s["v_ev"], 1)

            def statistics(b):
                wait(dve, "y_ok", 1, b, 1)
                for t in range(LT):
                    ins = dve.bn_stats(stats[:, t, :], y[:, t, :])
                ins.then_inc(s["ln_stat"], 1)

            def moments(b):
                hold(dve, "ln_stat", 1, b, 1)
                for t in range(LT):
                    ins = dve.bn_aggr(mv[:, t, :], stats[:, t, :])
                ins.then_inc(s["ln_aggr"], 1)

            def normalize(b):
                wait(dve, "ln_pow", 1, b, 1)
                wait(dve, "scattered", 16 * TOPK * LT, b, 0)
                wait(dve, "x_kept", 1, b, 0)
                for t in range(LT):
                    ins = dve.tensor_scalar(rows_s[:, t, 0:P], y[:, t, :], mv[:, t, 0:1], rstd[:, t:t + 1],
                                            ALU.subtract, ALU.mult)
                ins.then_inc(s["xn_ok"], 1)

            def over(v, shape):
                return v.broadcast_to(shape)

            tile8 = [P, LT, EXP]

            def take_logits(b):
                wait(dve, "lg_mm", 1, b, 1)
                dve.tensor_tensor(lg[:, :, :], misc[:, 1, 0:LT * EXP].rearrange("p (t e) -> p t e", e=EXP),
                                  over(br_bc[:, :].unsqueeze(1), tile8), ALU.add).then_inc(s["lg_ok"], 1)

            def largest(b):
                hold(dve, "lg_ok", 1, b, 1)
                for t in range(LT):
                    ins = dve.max(top8[:, t, :], lg[:, t, :])
                ins.then_inc(s["top_ok"], 1)

            def which(b):
                hold(dve, "top_ok", 1, b, 1)
                for t in range(LT):
                    ins = dve.max_index(idx8[:, t, :], top8[:, t, :], lg[:, t, :])
                ins.then_inc(s["idx_ok"], 1)

            def chosen(b):
                wait(dve, "idx_ok", 1, b, 1)
                for k in range(TOPK):
                    ins = dve.tensor_tensor(hot[:, k, :, :], over(iota[:, :].unsqueeze(1), tile8),
                                            over(idx8[:, :, k:k + 1], tile8), ALU.is_equal)
                ins.then_inc(s["hot_ok"], 1)

            def pick_both(b):
                wait(dve, "hot_ok", 1, b, 1)
                dve.tensor_tensor(picks[:, :], hot[:, 0, :, :].rearrange("p t e -> p (t e)"),
                                  hot[:, 1, :, :].rearrange("p t e -> p (t e)"), ALU.add).then_inc(s["picked"], 1)
                bb = best[:, b * LT:(b + 1) * LT, :] if isinstance(b, int) else best[:, bass.ds(b * LT, LT), :]
                dve.tensor_copy(bb, top8[:, :, 0:TOPK])
                dve.tensor_copy(rows_s[:, :, P:P + 1], idx8[:, :, 0:1])
                dve.tensor_scalar(rows_s[:, :, P + 1:XW], rows_s[:, :, P + 1:XW], float(LEN), None, ALU.add)\
                    .then_inc(s["meta"], 1)

            n_picks = LT * EXP

            def take_ranks(b):
                wait(dve, "rk_mm", 1, b, 1)
                wait(dve, "based", 1, b, 0)
                dve.tensor_tensor(slot_m[:, :, :], misc[:, 1, 0:n_picks].rearrange("p (t e) -> p t e", e=EXP),
                                  over(base[:, :].unsqueeze(1), tile8), ALU.add).then_inc(s["slot_ok"], 1)

            def slots_of_picks(b):
                wait(dve, "slot_ok", 1, b, 1)
                dve.tensor_tensor(base[:, :], misc[:, 1, n_picks:n_picks + EXP], base[:, :], ALU.add)\
                    .then_inc(s["based"], 1)
                for k in range(TOPK):
                    ins = dve.tensor_tensor(slot_k[:, k, :, :], hot[:, k, :, :], slot_m[:, :, :], ALU.mult)
                ins.then_inc(s["slotk_ok"], 1)

            def slot_numbers(b):
                wait(dve, "slotk_ok", 1, b, 1)
                with nc.allow_low_precision(reason="one whole number among zeros, kept exactly"):
                    dve.tensor_reduce(slots[:, :, :], slot_k[:, :, :, :], AX.X, ALU.add).then_inc(s["slots_ok"], 1)

            def residual(b):
                wait(dve, "wo_mm", 1, b, 1)
                dve.wait_ge(s["bo_ok"], BATCH)
                dve.wait_ge(s["wload"], 16 * N_WLOADS)
                xb = x_all[:, b * LT:(b + 1) * LT, :] if isinstance(b, int) else x_all[:, bass.ds(b * LT, LT), :]
                dve.tensor_tensor(y[:, :, :], misc[:, 1, :].rearrange("p (t d) -> p t d", t=LT), xb, ALU.add)\
                    .then_inc(s["y_ok"], 1)

            dve.wait_ge(s["v_zero"], 2)
            dve.wait_ge(s["consts"], 1 + LT)
            v_evac(0, 1)
            dve.wait_ge(s["raw_T"], 2)
            dve.tensor_copy(woT[:, :], misc[:, 0, 0:P]).then_inc(s["raw_ev"], 1)

            BEFORE_ROUND = ((6, moments), (10, take_logits), (11, chosen), (13, slots_of_picks))
            AFTER_ROUND = ((5, residual), (10, largest), (13, slot_numbers))
            AFTER_SQUARE = ((5, statistics), (7, normalize), (10, which), (11, pick_both), (12, take_ranks))

            def body(b, ph):
                first = isinstance(b, int) and b == 0
                last = isinstance(b, int) and b == BATCH - 1
                for u in range(UNITS):
                    for step, piece in (() if first else BEFORE_ROUND):
                        if u == step:
                            piece(b - 1)
                    round_turns(b, ph, u)
                    if u == 11:
                        kvT_evac(b)
                    for step, piece in (() if first else AFTER_ROUND):
                        if u == step:
                            piece(b - 1)
                    if u == 14:
                        c_evac(b)
                    if not (first and u < 2):
                        square(b, u - 2)
                    for step, piece in (() if first else AFTER_SQUARE):
                        if u == step:
                            piece(b - 1)
                    if u == 1 and not last:
                        x_evac(b + 1)
                    if u == 12:
                        kv_evac(b)
                    if u == 15 and not last:
                        v_evac(b + 1, 0)

            sequences(dve, body)
            e = BATCH
            square(e, -2)
            square(e, -1)
            for piece in (residual, statistics, moments, normalize, take_logits, largest, which, chosen, pick_both,
                          take_ranks, slots_of_picks, slot_numbers):
                piece(e - 1)

            n_rt = [0]

            def rchain(ins):
                n_rt[0] += 1
                ins.then_inc(s["rt"], 1)
                dve.wait_ge(s["rt"], n_rt[0])

            dve.wait_ge(s["based"], BATCH)
            dve.wait_ge(s["out_ev"], BATCH)
            cnt, full, cum_a, cum_b = (tiles_f[:, k, :] for k in range(4))
            dve.tensor_copy(ends_u[:, :], base[:, :]).then_inc(s["pads_at"], 1)
            rchain(dve.tensor_tensor(cnt, base[:, :], base_0[:, :], ALU.subtract))
            rchain(dve.tensor_scalar(cnt, cnt, 1.0 / P, MAGIC_LAST, ALU.mult, ALU.add))
            rchain(dve.tensor_scalar(full, cnt, MAGIC, -MAGIC, ALU.add, ALU.add))
            src, dst = full, cum_a
            for d in (1, 2, 4):
                dve.tensor_copy(dst[:, 0:d], src[:, 0:d])
                rchain(dve.tensor_tensor(dst[:, d:EXP], src[:, d:EXP], src[:, 0:EXP - d], ALU.add))
                src, dst = dst, (cum_b if dst is cum_a else cum_a)
            cube = [P, N_TILES, EXP]
            rchain(dve.tensor_tensor(ended, over(tile_no[:, :].unsqueeze(2), cube), over(src.unsqueeze(1), cube),
                                     ALU.is_ge))
            e_f, start_f, in_use, e_w, row_f, spare_f = (tab_f[:, k, :] for k in range(6))
            rchain(dve.tensor_scalar(spare_f, tile_no[:, :], float(P), None, ALU.mult))
            rchain(dve.tensor_reduce(e_f, ended, AX.X, ALU.add))
            rchain(dve.tensor_tensor(ended, ended, over(full.unsqueeze(1), cube), ALU.mult))
            rchain(dve.tensor_reduce(start_f, ended, AX.X, ALU.add))
            rchain(dve.tensor_tensor(start_f, tile_no[:, :], start_f, ALU.subtract))
            rchain(dve.tensor_scalar(in_use, e_f, float(EXP), float(P), ALU.is_lt, ALU.mult))
            rchain(dve.tensor_tensor(start_f, start_f, in_use, ALU.mult))
            rchain(dve.scalar_tensor_tensor(out=row_f, in0=e_f, scalar=float(REGION), in1=start_f,
                                            op0=ALU.mult, op1=ALU.add))
            rchain(dve.tensor_scalar(e_w, e_f, float(EXP - 1), None, ALU.min))
            dve.tensor_copy(tab_row, row_f).then_inc(s["tab_ok"], 1)
            dve.tensor_copy(tab_e, e_w).then_inc(s["tab_ok"], 1)
            dve.tensor_tensor(gate[:, 0, :], best[:, :, 1], best[:, :, 0], ALU.subtract).then_inc(s["gap_ok"], 1)
            dve.wait_ge(s["gap_exp"], 1)
            rchain(dve.tensor_scalar(gate[:, 2, :], gate[:, 1, :], 1.0, None, ALU.add))
            rchain(dve.reciprocal(gate[:, 2, :], gate[:, 2, :]))
            dve.tensor_tensor(gate[:, 3, :], gate[:, 1, :], gate[:, 2, :], ALU.mult).then_inc(s["gates_ok"], 1)
            dve.wait_ge(s["tab_ok"], 2)

            def pick(v, i, r, w):
                n = i * UNROLL + r
                return v[:, n * w:(n + 1) * w] if isinstance(n, int) else v[:, bass.ds(n * w, w)]

            def x_evac_tile(i, r):
                wait(dve, "xT_t", UNROLL, i, r + 1)
                wait(dve, "h_t", UNROLL, i, r - 1)
                dve.tensor_copy(xgT[:, r % 2, :], xT_bank[r % 2][:, 0:P]).then_inc(s["xT_e"], 1)

            def relu(i, r):
                wait(dve, "h_t", UNROLL, i, r + 1)
                wait(dve, "y_t", UNROLL, i, r - 1)
                cube = [P, HT, P]
                dve.tensor_tensor(hidT[:, r % 2, :].rearrange("p (j n) -> p j n", j=HT),
                                  h_bank[r % 2].rearrange("p (j n) -> p j n", j=HT),
                                  over(w_now[:, r % W_RING, AT_B1:WROW].unsqueeze(2), cube), ALU.max)\
                    .then_inc(s["h_e"], 1)

            def target_1(i, r):
                wait(dve, x_in_sem[r % RING_X], 16, i, 16)
                wait(dve, y_sem[r], 16, i, 0)
                dve.tensor_tensor(first_pick[:, r, :], xg[:, r, P:P + 1], pick(e_w, i, r, 1), ALU.is_equal)
                dve.scalar_tensor_tensor(out=spare[:, r, :], in0=xg[:, r, P:P + 1], scalar=0.0,
                                         in1=pick(spare_f, i, r, 1), op0=ALU.is_lt, op1=ALU.mult)\
                    .then_inc(s["pick1"], 1)

            def target_2(i, r):
                wait(dve, "pick1", UNROLL, i, r + 1)
                dve.scalar_tensor_tensor(out=first_pick[:, r, :], in0=first_pick[:, r, :], scalar=-float(ROWS),
                                         in1=xg[:, r, P + 1:XW], op0=ALU.mult, op1=ALU.add)\
                    .then_inc(s["pick2"], 1)

            def target_3(i, r):
                wait(dve, "pick2", UNROLL, i, r + 1)
                dve.tensor_tensor(y_at[:, r, :], first_pick[:, r, :], spare[:, r, :], ALU.add)\
                    .then_inc(s["y_at_ok"], 1)

            def output(i, r):
                wait(dve, "y_t", UNROLL, i, r + 1)
                dve.tensor_tensor(y_row[:, r, :], y_bank[r % 2][:, 0:P], w_now[:, r % W_RING, AT_B2:AT_B1], ALU.add)\
                    .then_inc(s["y_e"], 1)

            def steps(i, head, tail):
                for r in range(UNROLL):
                    if not tail:
                        target_1(i, r)
                        relu(i, r)
                        target_2(i, r)
                    if not (head and r < 1) and not (tail and r > 0):
                        output(*back(i, r, 1))
                    if not tail:
                        target_3(i, r)
                        if not (r >= UNROLL - 2 and isinstance(i, int) and i == N_TILES // UNROLL - 1):
                            x_evac_tile(*((i, r + 2) if r < UNROLL - 2 else (i + 1, r + 2 - UNROLL)))

            x_evac_tile(0, 0)
            x_evac_tile(0, 1)
            tile_steps(dve, steps)

            for n in range(BATCH):
                r = n % 2
                dve.wait_ge(s["sum1"], n + 1)
                if n >= 2:
                    dve.wait_ge(s["fin_ok"], n - 1)
                for t in range(LT):
                    ins = dve.scalar_tensor_tensor(out=y_sum[:, r, t, :], in0=y_back[:, n % Y_RING, 1, t, :],
                                                   scalar=gate_of(1, n, t), in1=y_back[:, n % Y_RING, 0, t, :],
                                                   op0=ALU.mult, op1=ALU.add)
                ins.then_inc(s["sum2"], 1)
                dve.wait_ge(s["sum2"], n + 1)
                for t in range(LT):
                    ins = dve.bn_stats(stats_f[:, r, t, :], y_sum[:, r, t, :])
                ins.then_inc(s["fin_stat"], 1)
                dve.wait_ge(s["fin_stat"], n + 1)
                for t in range(LT):
                    ins = dve.bn_aggr(mv_f[:, r, t, :], stats_f[:, r, t, :])
                ins.then_inc(s["fin_aggr"], 1)

        @block.gpsimd
        def _(pool):
            pool.memset(v_pad[:, :, :, :], 0.0).then_inc(s["v_zero"], 1)
            pool.memset(kv_pad[:, :, :, :], 0.0).then_inc(s["v_zero"], 1)

            def square(b, u):
                if u % UNITS not in POOL_SQ:
                    return
                wait(pool, "sines", UNITS, b, u + 1)
                f = feats[:, u % HALF, 1, :]
                pool.tensor_tensor(f, f, f, ALU.mult).then_inc(s["sq_p"], 1)

            def rsqrt(per, n, base):
                wait(pool, "ln_aggr", per, n, base + 1)
                pool.tensor_tensor(rstd[:, :], mv[:, :, 1], eps_t[:, :], ALU.add).then_inc(s["ln_eps"], 1)
                wait(pool, "ln_eps", per, n, base + 1)
                pool.tensor_tensor(rstd[:, :], rstd[:, :], half_t[:, :], ALU.pow).then_inc(s["ln_pow"], 1)


            def body(b, ph):
                first = isinstance(b, int) and b == 0
                last = isinstance(b, int) and b == BATCH - 1
                for u in range(UNITS):
                    if not (first and u < 2):
                        square(b, u - 2)
                    if first and u >= HALF:
                        pool.wait_ge(s["xload"], 16 * BATCH)
                        t = (u - HALF) * LT
                        xb = x_all[:, t:t + LT, :]
                        pool.tensor_tensor(xb, xb, bo_bc[:, :, :], ALU.add).then_inc(s["bo_ok"], 1)
                    if u == 6 and not first:
                        rsqrt(1, b - 1, 0)
                    if u in (7, 9) and not last:
                        split(pool, b + 1, (u - 7) // 2)
                    if u in (14, 15) and not first:
                        send_rows(b - 1, u - 14)

            def send_rows(b, k):
                hold(pool, "slots_ok", 1, b, 1)
                hold(pool, "meta", 1, b, 1)
                for t in range(LT):
                    pool.indirect_dma_start(routed_dram, bass.IndirectOffsetOnAxis(slots[:, k, t:t + 1], 0),
                                            rows_s[:, t, :], None).then_inc(s["scattered"], 16)

            sequences(pool, body)
            square(BATCH, -2)
            square(BATCH, -1)
            rsqrt(1, BATCH - 1, 0)
            for k in range(TOPK):
                send_rows(BATCH - 1, k)

            def steps(i, head, tail):
                for r in range(UNROLL):
                    if not (head and r < 1) and not (tail and r > 0):
                        j, q = back(i, r, 1)
                        hold(pool, "y_e", UNROLL, j, q + 1)
                        hold(pool, "y_at_ok", UNROLL, j, q + 1)
                        pool.indirect_dma_start(expert_dram, bass.IndirectOffsetOnAxis(y_at[:, q, :], 0),
                                                y_row[:, q, :], None).then_inc(y_sem[q], 16)

            tile_steps(pool, steps)

            def scale_and_shift(n):
                r = n % 2
                pool.wait_ge(s["fin_aggr"], n + 1)
                pool.tensor_tensor(rstd_f[:, r, :], mv_f[:, r, :, 1], eps_t[:, :], ALU.add)\
                    .then_inc(s["fin_eps"], 1)
                pool.wait_ge(s["fin_eps"], n + 1)
                pool.tensor_tensor(rstd_f[:, r, :], rstd_f[:, r, :], half_t[:, :], ALU.pow)\
                    .then_inc(s["fin_rstd"], 1)
                pool.wait_ge(s["fin_rstd"], n + 1)
                pool.tensor_tensor(shift_f[:, r, :], mv_f[:, r, :, 0], rstd_f[:, r, :], ALU.mult)\
                    .then_inc(s["fin_mean"], 1)
                pool.wait_ge(s["fin_mean"], n + 1)
                pool.tensor_tensor(shift_f[:, r, :], zero_t[:, :], shift_f[:, r, :], ALU.subtract)\
                    .then_inc(s["fin_shift"], 1)

            def add_row(n):
                pool.wait_ge(s["first_ok"], n + 1)
                y_n = y_back[:, n % Y_RING, 0, :, :]
                pool.tensor_tensor(y_n, y_n, x_all[:, n * LT:(n + 1) * LT, :], ALU.add).then_inc(s["sum1"], 1)

            pool.wait_ge(s["x_kept"], BATCH)
            add_row(0)
            add_row(1)
            for n in range(BATCH):
                scale_and_shift(n)
                if n + 2 < BATCH:
                    add_row(n + 2)


_INS = ["attn_x", "attn_proj_mat", "attn_Wq", "attn_bq", "attn_Wk", "attn_bk", "attn_Wv", "attn_bv", "attn_Wo",
        "attn_bo", "ffn_W1", "ffn_b1", "ffn_W2", "ffn_b2", "ffn_Wr", "ffn_br"]


def constants():
    import numpy as np
    mask = np.zeros((STK, SPL), np.float32)
    for r in range(STK):
        mask[r, r // (SPL * DH)] = 1.0
    tri = np.triu(np.ones((P, P), np.float16), 1)
    tok = np.zeros((P, LT, 2), np.float32)
    tok[:, :, 1] = ROWS - LEN + np.arange(LT) * P + np.arange(P)[:, None]
    pad = np.zeros((P, XW), np.float32)
    pad[:, P] = -1.0
    pad[:, P + 1] = TOPK * ROWS + np.arange(P)
    return [np.eye(P, dtype=np.float32), -np.eye(P, dtype=np.float16), mask,
            np.arange(EXP, dtype=np.float32), np.arange(EXP, dtype=np.float32) * REGION,
            np.arange(N_TILES, dtype=np.float32), tri, tok, pad]


def kernel(**inputs):
    import numpy as _np
    import concourse.bacc as _bacc
    from concourse import mybir as _mybir
    from concourse.bass_utils import run_bass_kernel_spmd as _run

    nc = _bacc.Bacc("TRN2", target_bir_lowering=False, num_devices=1)
    arrays, args = {}, []
    every = [(n, _np.ascontiguousarray(inputs["L0_" + n])) for n in _INS]
    every += [(f"const{i}", c) for i, c in enumerate(constants())]
    for name, a in every:
        arrays[name] = a
        args.append(nc.dram_tensor(name, a.shape, _mybir.dt.from_np(a.dtype), kind="ExternalInput").ap())
    args.append(nc.dram_tensor("out", (BATCH, LEN, P), F32, kind="ExternalOutput").ap())
    build(nc, *args)
    r = _run(nc, [arrays], core_ids=[0])
    return r.results[0]["out"]
```
